# Optimizing a Trainium2 kernel written in Bass

```python
import numpy as np
import jax
import jax.numpy as jnp

def _softmax(x, axis=-1):
    return jax.nn.softmax(x, axis=axis)

def _gelu(x):
    return jax.nn.gelu(x, approximate=True)

def _silu(x):
    return jax.nn.silu(x)

def _sigmoid(x):
    return jax.nn.sigmoid(x)

def _layernorm(x, axis=-1, eps=1e-05):
    m = jnp.mean(x, axis=axis, keepdims=True)
    v = jnp.var(x, axis=axis, keepdims=True)
    return (x - m) / jnp.sqrt(v + eps)

def _scatter_add(tgt, idx, src, axis=0):
    return tgt.at[idx].add(src)

def _segment_sum(src, seg, n):
    return jax.ops.segment_sum(src, seg, n)
kernel_name = 'mk_perceiver_d1_seqx_r8_c32f46'

def setup_inputs(seed: int=0):
    np.random.seed(seed)
    _w = jnp.asarray

    def _rec_inputs():
        import jax
        import jax.numpy as jnp
        _rk = jax.random.key(seed)
        x = -0.0002928 + 1 * jax.random.normal(jax.random.fold_in(_rk, 1), (128, 32, 128), jnp.float32)
        _lenS = 32 - jax.random.randint(jax.random.fold_in(_rk, 7), (128,), 0, max(1, 32 // 4) + 1, jnp.int32)
        _lenS2 = 257 - jax.random.randint(jax.random.fold_in(_rk, 8), (128,), 0, max(1, 257 // 4) + 1, jnp.int32)
        _ctx_1024P = jax.random.normal(jax.random.fold_in(_rk, 11), (128, 16, 128), jnp.float32)
        _ctx_1024c = jax.random.dirichlet(jax.random.fold_in(_rk, 511), 0.3 * jnp.ones((16,), jnp.float32), (128, 257))
        _ctx_1024t = jnp.einsum('bsk,bkd->bsd', _ctx_1024c, _ctx_1024P)
        _ctx_1024t = _ctx_1024t * jax.lax.rsqrt(jnp.mean(jnp.square(_ctx_1024t)) + 1e-12) * 0.953939
        ctx_1024 = -1.39393e-06 + 0.999914 * (_ctx_1024t + 0.3 * jax.random.normal(jax.random.fold_in(_rk, 611), (128, 257, 128), jnp.float32))
        _validS = jnp.arange(32)[None, :] < _lenS[:, None]
        _validS2 = jnp.arange(257)[None, :] < _lenS2[:, None]
        _causal = jnp.tril(jnp.ones((32, 32), dtype=bool))
        mask_Bx1x1xS2_if1 = jnp.where(jnp.ones((128, 1, 1, 257), dtype=bool), 1, 0).astype(jnp.int32)
        return (x, ctx_1024, mask_Bx1x1xS2_if1)
    x, ctx_1024, mask_Bx1x1xS2_if1 = _rec_inputs()

    def _L0_xattn_setup():
        import jax, jax.numpy as jnp
        import numpy as np
        D_MODEL = 128
        N_HEAD = 16

        def _split(x, n_head):
            B, S, D = x.shape
            return x.reshape(B, S, n_head, D // n_head).transpose(0, 2, 1, 3)
        key = jax.random.key(seed)
        ks = jax.random.split(key, 12)
        B, S, D = (2, 256, D_MODEL)
        std = 1.0 / np.sqrt(D)
        inp = {'Q': jax.random.normal(ks[0], (B, S, D), jnp.float32), 'K': jax.random.normal(ks[1], (B, S, D), jnp.float32), 'V': jax.random.normal(ks[2], (B, S, D), jnp.float32), 'mask': jnp.ones((B, 1, 1, S), jnp.int32), 'Wq': jax.random.normal(ks[3], (D, D), jnp.float32) * std, 'bq': jax.random.normal(ks[4], (D,), jnp.float32) * std, 'Wk': jax.random.normal(ks[5], (D, D), jnp.float32) * std, 'bk': jax.random.normal(ks[6], (D,), jnp.float32) * std, 'Wv': jax.random.normal(ks[7], (D, D), jnp.float32) * std, 'bv': jax.random.normal(ks[8], (D,), jnp.float32) * std, 'Wo': jax.random.normal(ks[9], (D, D), jnp.float32) * std, 'bo': jax.random.normal(ks[10], (D,), jnp.float32) * std}
        return inp
    _L0_xattn_all = _L0_xattn_setup()
    _L0_xattn_in = {k: v for k, v in _L0_xattn_all.items() if k in ('Wq', 'bq', 'Wk', 'bk', 'Wv', 'bv', 'Wo', 'bo')}
    del _L0_xattn_all

    def _L0_attn_setup():
        import jax, jax.numpy as jnp
        import numpy as np
        from math import sqrt
        EMBED = 128
        HEADS = 16
        key = jax.random.key(seed)
        k1, k2, k3, k4, k5 = jax.random.split(key, 5)
        x = jax.random.normal(k1, (2, 256, EMBED), dtype=jnp.float32)
        s = 1.0 / sqrt(EMBED)
        W_qkv = jax.random.normal(k2, (EMBED, 3 * EMBED), dtype=jnp.float32) * s
        b_qkv = jax.random.normal(k3, (3 * EMBED,), dtype=jnp.float32) * 0.01
        W_out = jax.random.normal(k4, (EMBED, EMBED), dtype=jnp.float32) * s
        b_out = jax.random.normal(k5, (EMBED,), dtype=jnp.float32) * 0.01
        return {'x': x, 'W_qkv': W_qkv, 'b_qkv': b_qkv, 'W_out': W_out, 'b_out': b_out}
    _L0_attn_all = _L0_attn_setup()
    _L0_attn_in = {k: v for k, v in _L0_attn_all.items() if k in ('W_qkv', 'b_qkv', 'W_out', 'b_out')}
    del _L0_attn_all

    def _L0_ffn_setup():
        import jax, jax.numpy as jnp
        import numpy as np
        L, E, H, F, K = (4, 4, 128, 512, 2)
        B, S = (4, 256)
        EPS = 1e-05

        def _moe_layer(x, rw, rb, g, b, w1, b1, w2, b2):
            logits = jnp.einsum('bsh,he->bse', x, rw) + rb
            probs = jax.nn.softmax(logits, axis=-1)
            vals, idx = jax.lax.top_k(probs, K)
            vals = vals / vals.sum(axis=-1, keepdims=True)
            mu = x.mean(axis=-1, keepdims=True)
            xc = x - mu
            xhat = xc * jax.lax.rsqrt((xc * xc).mean(axis=-1, keepdims=True) + EPS)
            xe = xhat[None] * g[:, None, None, :] + b[:, None, None, :]
            h = jax.nn.gelu(jnp.einsum('ebsh,ehf->ebsf', xe, w1) + b1[:, None, None, :], approximate=False)
            y = jnp.einsum('ebsf,efh->ebsh', h, w2) + b2[:, None, None, :]
            expert_out = x[None] + y
            comb = jnp.einsum('bsk,bske->bse', vals, jax.nn.one_hot(idx, E, dtype=x.dtype))
            return jnp.einsum('bse,ebsh->bsh', comb, expert_out)
        key = jax.random.key(seed)
        ks = jax.random.split(key, 4)
        return {'hidden_states': jax.random.normal(ks[0], (B, S, H), jnp.float32), 'router_w': 0.02 * jax.random.normal(ks[1], (L, H, E), jnp.float32), 'router_b': jnp.zeros((L, E), jnp.float32), 'ln_g': jnp.ones((L, E, H), jnp.float32), 'ln_b': jnp.zeros((L, E, H), jnp.float32), 'w1': 0.02 * jax.random.normal(ks[2], (L, E, H, F), jnp.float32), 'b1': jnp.zeros((L, E, F), jnp.float32), 'w2': 0.02 * jax.random.normal(ks[3], (L, E, F, H), jnp.float32), 'b2': jnp.zeros((L, E, H), jnp.float32)}
    _L0_ffn_all = _L0_ffn_setup()
    _L0_ffn_in = {k: v for k, v in _L0_ffn_all.items() if k in ('router_w', 'router_b', 'ln_g', 'ln_b', 'w1', 'b1', 'w2', 'b2')}
    del _L0_ffn_all
    return {'x': x, 'ctx_1024': ctx_1024, 'mask_Bx1x1xS2_if1': mask_Bx1x1xS2_if1, 'L0_xattn_Wq': _L0_xattn_in['Wq'], 'L0_xattn_bq': _L0_xattn_in['bq'], 'L0_xattn_Wk': _L0_xattn_in['Wk'], 'L0_xattn_bk': _L0_xattn_in['bk'], 'L0_xattn_Wv': _L0_xattn_in['Wv'], 'L0_xattn_bv': _L0_xattn_in['bv'], 'L0_xattn_Wo': _L0_xattn_in['Wo'], 'L0_xattn_bo': _L0_xattn_in['bo'], 'L0_attn_W_qkv': _L0_attn_in['W_qkv'], 'L0_attn_b_qkv': _L0_attn_in['b_qkv'], 'L0_attn_W_out': _L0_attn_in['W_out'], 'L0_attn_b_out': _L0_attn_in['b_out'], 'L0_ffn_router_w': _L0_ffn_in['router_w'], 'L0_ffn_router_b': _L0_ffn_in['router_b'], 'L0_ffn_ln_g': _L0_ffn_in['ln_g'], 'L0_ffn_ln_b': _L0_ffn_in['ln_b'], 'L0_ffn_w1': _L0_ffn_in['w1'], 'L0_ffn_b1': _L0_ffn_in['b1'], 'L0_ffn_w2': _L0_ffn_in['w2'], 'L0_ffn_b2': _L0_ffn_in['b2']}

def reference(x, ctx_1024, mask_Bx1x1xS2_if1, L0_xattn_Wq, L0_xattn_bq, L0_xattn_Wk, L0_xattn_bk, L0_xattn_Wv, L0_xattn_bv, L0_xattn_Wo, L0_xattn_bo, L0_attn_W_qkv, L0_attn_b_qkv, L0_attn_W_out, L0_attn_b_out, L0_ffn_router_w, L0_ffn_router_b, L0_ffn_ln_g, L0_ffn_ln_b, L0_ffn_w1, L0_ffn_b1, L0_ffn_w2, L0_ffn_b2):
    import jax
    import jax.numpy as jnp

    def _L0_xattn_ref(Q, K, V, mask, Wq, bq, Wk, bk, Wv, bv, Wo, bo):
        import jax, jax.numpy as jnp
        import numpy as np
        D_MODEL = 128
        N_HEAD = 16

        def _split(x, n_head):
            B, S, D = x.shape
            return x.reshape(B, S, n_head, D // n_head).transpose(0, 2, 1, 3)
        q = _split(Q @ Wq.T + bq, N_HEAD)
        k = _split(K @ Wk.T + bk, N_HEAD)
        v = _split(V @ Wv.T + bv, N_HEAD)
        d_head = k.shape[-1]
        scale = 1.0 / jnp.sqrt(jnp.asarray(d_head, q.dtype))
        score = jnp.einsum('bhqd,bhkd->bhqk', q, k) * scale
        score = jnp.where(mask == 0, -jnp.inf, score)
        attn = jax.nn.softmax(score, axis=-1)
        out = jnp.einsum('bhqk,bhkd->bhqd', attn, v)
        B, H, S, dh = out.shape
        out = out.transpose(0, 2, 1, 3).reshape(B, S, H * dh)
        return out @ Wo.T + bo

    def _L0_attn_ref(x, W_qkv, b_qkv, W_out, b_out):
        import jax, jax.numpy as jnp
        import numpy as np
        from math import sqrt
        EMBED = 128
        HEADS = 16
        B, N, E = x.shape
        H = HEADS
        d = E // H
        qkv = x @ W_qkv + b_qkv
        q, k, v = jnp.split(qkv, 3, axis=2)
        q = q.reshape(B, N, H, d)
        k = k.reshape(B, N, H, d)
        v = v.reshape(B, N, H, d)
        energy = jnp.einsum('bqhe,bkhe->bqhk', q, k)
        attn = jax.nn.softmax(energy, axis=-1) / sqrt(E)
        out = jnp.einsum('bihv,bvhd->bihd', attn, v)
        out = out.reshape(B, N, E)
        return out @ W_out + b_out

    def _L0_ffn_ref(hidden_states, router_w, router_b, ln_g, ln_b, w1, b1, w2, b2):
        import jax, jax.numpy as jnp
        import numpy as np
        L, E, H, F, K = (4, 4, 128, 512, 2)
        B, S = (4, 256)
        EPS = 1e-05

        def _moe_layer(x, rw, rb, g, b, w1, b1, w2, b2):
            logits = jnp.einsum('bsh,he->bse', x, rw) + rb
            probs = jax.nn.softmax(logits, axis=-1)
            vals, idx = jax.lax.top_k(probs, K)
            vals = vals / vals.sum(axis=-1, keepdims=True)
            mu = x.mean(axis=-1, keepdims=True)
            xc = x - mu
            xhat = xc * jax.lax.rsqrt((xc * xc).mean(axis=-1, keepdims=True) + EPS)
            xe = xhat[None] * g[:, None, None, :] + b[:, None, None, :]
            h = jax.nn.gelu(jnp.einsum('ebsh,ehf->ebsf', xe, w1) + b1[:, None, None, :], approximate=False)
            y = jnp.einsum('ebsf,efh->ebsh', h, w2) + b2[:, None, None, :]
            expert_out = x[None] + y
            comb = jnp.einsum('bsk,bske->bse', vals, jax.nn.one_hot(idx, E, dtype=x.dtype))
            return jnp.einsum('bse,ebsh->bsh', comb, expert_out)
        x = hidden_states
        for l in range(L):
            x = _moe_layer(x, router_w[l], router_b[l], ln_g[l], ln_b[l], w1[l], b1[l], w2[l], b2[l])
        return x
    x = x + _L0_xattn_ref(_layernorm(x, axis=-1), ctx_1024, ctx_1024, mask_Bx1x1xS2_if1, L0_xattn_Wq, L0_xattn_bq, L0_xattn_Wk, L0_xattn_bk, L0_xattn_Wv, L0_xattn_bv, L0_xattn_Wo, L0_xattn_bo)
    x = x + _L0_attn_ref(_layernorm(x, axis=-1), L0_attn_W_qkv, L0_attn_b_qkv, L0_attn_W_out, L0_attn_b_out)
    x = x + _L0_ffn_ref(_layernorm(x, axis=-1), L0_ffn_router_w, L0_ffn_router_b, L0_ffn_ln_g, L0_ffn_ln_b, L0_ffn_w1, L0_ffn_b1, L0_ffn_w2, L0_ffn_b2)
    return x

_drawn_inputs = setup_inputs


def setup_inputs(seed=0):
    import zlib

    import numpy as np

    out = dict(_drawn_inputs(seed))
    spreads = {'L0_ffn_router_b': (0.0, 0.1),
     'L0_ffn_ln_g': (1.0, 0.6),
     'L0_ffn_ln_b': (0.0, 0.8),
     'L0_ffn_b1': (0.0, 0.461),
     'L0_ffn_b2': (0.0, 0.1)}
    factors = {'L0_xattn_bq': 2.869, 'L0_xattn_bk': 64.0, 'L0_attn_b_qkv': 42.107, 'L0_attn_b_out': 5.596}
    for name, (base, spread) in spreads.items():
        noise = np.random.default_rng([zlib.crc32(name.encode()), seed]).standard_normal(out[name].shape)
        drawn = base * np.exp(spread * noise) if base else spread * noise
        out[name] = jnp.asarray(drawn.astype(out[name].dtype))
    for name, factor in factors.items():
        out[name] = (out[name] * factor).astype(out[name].dtype)
    return out
```

```python
from contextlib import ExitStack

import concourse.bass as bass
from concourse import mybir

F32 = mybir.dt.float32
F16 = mybir.dt.float16
I32 = mybir.dt.int32
ALU = mybir.AluOpType
ACT = mybir.ActivationFunctionType
AX = mybir.AxisListType

P = 128
D = 128
H = 16
DH = D // H
G = 4
GH = H // G
GD = GH * DH
SQ = 32
EPS = 1e-5
MASKED = -60000.0
RSQRT_SEED = float(0x5F3759DF)


def wait(eng, sem, value):
    if not isinstance(value, int) or value > 0:
        eng.wait_ge(sem, value)


def emit_rstd(dve, rstd, work, var, done, base):
    dve.tensor_scalar(work, var, EPS, None, ALU.add).then_inc(done, 1)
    dve.wait_ge(done, base + 1)
    dve.tensor_scalar(rstd.bitcast(I32), work.bitcast(I32), 1, None, ALU.logical_shift_right).then_inc(done, 1)
    dve.wait_ge(done, base + 2)
    dve.tensor_scalar(rstd.bitcast(I32), rstd.bitcast(I32), -1.0, RSQRT_SEED, ALU.mult, ALU.add).then_inc(done, 1)
    return base + 3


def newton(dve, rstd, work, tmp, done, base):
    for k in range(3):
        dve.wait_ge(done, base + 3 * k)
        dve.tensor_tensor(tmp, rstd, rstd, ALU.mult).then_inc(done, 1)
        dve.wait_ge(done, base + 3 * k + 1)
        dve.scalar_tensor_tensor(tmp, tmp, -0.5, work, ALU.mult, ALU.mult).then_inc(done, 1)
        dve.wait_ge(done, base + 3 * k + 2)
        dve.scalar_tensor_tensor(rstd, tmp, 1.5, rstd, ALU.add, ALU.mult).then_inc(done, 1)
    return base + 9


RSTD_STEPS = 12


def inverse_deviation(dve, rstd, work, tmp, var, done, base):
    newton(dve, rstd, work, tmp, done, emit_rstd(dve, rstd, work, var, done, base))
    dve.wait_ge(done, base + RSTD_STEPS)


def build(nc, x, ctx, mask, Wq, bq, Wk, bk, Wv, bv, Wo, bo, W_qkv, b_qkv, W_out, b_out,
          router_w, router_b, ln_g, ln_b, w1, b1, w2, b2, out):
    B, _, _ = x.shape
    SK = ctx.shape[1]
    KM = SK - 1
    KC = KM // P
    T = B * SQ
    NT = T // P
    PB = P // SQ
    NPACK = B // PB
    NPAIR = PB // 2
    CW = GD + 1
    SCALE = float(DH) ** -0.5

    x_tiles = x.rearrange("b q c -> (b q) c").rearrange("(t p) c -> p t c", p=P)
    out_tiles = out.rearrange("b q c -> (b q) c").rearrange("(t p) c -> p t c", p=P)
    mask_d = mask.rearrange("b a c k -> (b a c) k")

    PARTS = 3
    q_d = nc.dram_tensor("q_parts_dram", [G, GD, PARTS, T], F16, kind="Internal").ap()
    k_d = nc.dram_tensor("k_parts_dram", [2, GD, PARTS, G, PB * KM], F16, kind="Internal").ap()
    kl_d = nc.dram_tensor("last_k_parts_dram", [GD, PARTS, G, B], F16, kind="Internal").ap()
    bias_d = nc.dram_tensor("mask_bias_dram", [B, KM], F16, kind="Internal").ap()
    biasl_d = nc.dram_tensor("last_mask_bias_dram", [B], F16, kind="Internal").ap()
    vlast_d = nc.dram_tensor("last_values_dram", [B, G * CW], F32, kind="Internal").ap()

    with ExitStack() as whole:
        def sb(scope, name, shape, dt):
            return scope.enter_context(nc.sbuf_tensor(name, shape, dt))

        def sem(name):
            return whole.enter_context(nc.semaphore(name))

        bank = [whole.enter_context(nc.psum_tensor(f"bank{i}", [P, 512], F32)) for i in range(8)]
        xs = sb(whole, "xs", [P, NT, D], F32)
        ident = sb(whole, "ident", [P, P], F32)
        WoM = sb(whole, "WoM", [P, GH, D], F32)
        rowsel = sb(whole, "rowsel", [P, GH], F32)

        cross = whole.enter_context(ExitStack())
        WkT = sb(cross, "WkT", [P, D], F32)
        WvT = sb(cross, "WvT", [P, D], F32)
        bk_c = sb(cross, "bk_c", [P, 1], F32)
        maskT = sb(cross, "maskT", [P, KC, B], F16)
        KL = sb(cross, "KL", [P, G, B], F16)
        NROW = PARTS * GD
        KROW, SROW = NROW + 1, NROW + 2
        KS = [sb(cross, f"KS{i}", [P, G, PB, KM], F16) for i in range(4)]
        QS = [sb(cross, f"QS{i}", [P, G, GH, SQ, PB], F16) for i in range(4)]
        VX = [sb(cross, f"VX{i}", [P, PB, KC, 2, G, CW], F16) for i in range(4)]
        VL = [sb(cross, f"VL{i}", [P, PB, G, CW], F32) for i in range(4)]

        A = ExitStack()
        with A:
            w_nat = sb(A, "w_nat", [P, 4, D], F32)
            WqT = sb(A, "WqT", [P, D], F32)
            WoT = sb(A, "WoT", [P, D], F32)
            bq_c = sb(A, "bq_c", [P, 1], F32)
            bv_c = sb(A, "bv_c", [P, 1], F32)
            bvR = sb(A, "bvR", [P, D], F32)
            boR = sb(A, "boR", [P, D], F32)
            mask_i = sb(A, "mask_i", [P, SK], I32)
            m01 = sb(A, "m01", [P, SK], F32)
            bias16 = sb(A, "bias16", [P, SK], F16)
            clast = sb(A, "clast", [P, D], F32)
            clT = sb(A, "clT", [P, D], F32)
            klh = sb(A, "klh", [P, B], F16)
            kll = sb(A, "kll", [P, B], F16)
            vlast = sb(A, "vlast", [P, G, CW], F32)
            sel3 = sb(A, "sel3", [P, GH, G], F32)
            stats = sb(A, "stats", [P, NT, 6], F32)
            mv = sb(A, "mv", [P, NT, 2], F32)
            rstd = sb(A, "rstd", [P, NT], F32)
            nwt = sb(A, "nwt", [P, NT], F32)
            nw2 = sb(A, "nw2", [P, NT], F32)
            xn = [sb(A, f"xn{i}", [P, 4, D], F32) for i in range(2)]
            xnT = [sb(A, f"xnT{i}", [P, 4 * P], F32) for i in range(2)]
            q32 = [sb(A, f"q32_{i}", [P, 4 * P], F32) for i in range(2)]
            qh = [sb(A, f"qh{i}", [P, 4 * P], F16) for i in range(2)]
            ql = [sb(A, f"ql{i}", [P, 4 * P], F16) for i in range(2)]

            a_x, a_w, a_out, a_kl = sem("a_x"), sem("a_w"), sem("a_out"), sem("a_kl")
            a_id, a_pool, a_fill = sem("a_id"), sem("a_pool"), sem("a_fill")
            a_wt, a_wtc, a_dve, a_pe = sem("a_wt"), sem("a_wtc"), sem("a_dve"), sem("a_pe")
            a_klh, a_last, a_kld = sem("a_klh"), sem("a_last"), sem("a_kld")
            a_st, a_ag, a_rs, a_xn = sem("a_st"), sem("a_ag"), sem("a_rs"), sem("a_xn")
            a_xT, a_xTc, a_q, a_q32, a_qh, a_ql = (sem("a_xT"), sem("a_xTc"), sem("a_q"),
                                                   sem("a_q32"), sem("a_qh"), sem("a_ql"))
            a_qd = [sem("a_qd0"), sem("a_qd1")]
            WD = 16 * 10

            def batch_first(t):
                return t[:, :].rearrange("p (k b q) -> p k q b", k=4, b=PB)

            def batch_last(t):
                return t[:, :].rearrange("p (k q b) -> p k q b", k=4, b=PB)

            with nc.Block() as block:
                @block.sync
                def _(sp):
                    sp.dma_start(xs[:, :, :], x_tiles).then_inc(a_x, 16)
                    for k, w in enumerate((Wq, Wk, Wv, Wo)):
                        sp.dma_start(w_nat[:, k, :], w).then_inc(a_w, 16)
                    for dst, src in ((bq_c, bq), (bk_c, bk), (bv_c, bv)):
                        sp.dma_start(dst[:, :], src.rearrange("(p a) -> p a", a=1)).then_inc(a_w, 16)
                    sp.dma_start(boR[:, :], bo.rearrange("(a n) -> a n", a=1).broadcast_to((P, D))).then_inc(a_w, 16)
                    sp.dma_start(mask_i[:, :], mask_d).then_inc(a_w, 16)
                    sp.dma_start(clast[:, :], ctx[:, KM, :]).then_inc(a_w, 16)
                    sp.wait_ge(a_dve, 4)
                    sp.dma_start(bias_d, bias16[:, 0:KM]).then_inc(a_out, 16)
                    sp.dma_start(biasl_d.rearrange("(b a) -> b a", a=1), bias16[:, KM:SK]).then_inc(a_out, 16)
                    for g in range(G):
                        sp.wait_ge(a_out, 32)
                        sp.dma_start(KL[NROW:KROW, g, :],
                                     biasl_d.rearrange("(a b) -> a b", a=1)).then_inc(a_kl, 16)
                    sp.wait_ge(a_last, 2)
                    for part, src in ((0, klh), (1, kll), (2, klh)):
                        sp.dma_start(kl_d[:, part, :, :].rearrange("i g b -> g i b"), src[:, :]).then_inc(a_kld, 16)
                    sp.wait_ge(a_kld, 16 * PARTS)
                    sp.dma_start(KL[0:NROW, :, :].rearrange("r g b -> r (g b)"),
                                 kl_d.rearrange("i s g b -> (i s) (g b)")).then_inc(a_kl, 16)
                    sp.wait_ge(a_last, 4)
                    sp.dma_start(vlast_d, vlast[:, :, :].rearrange("p g c -> p (g c)")).then_inc(a_out, 16)
                    with sp.Fori(0, NT // 8) as it:
                        for u in range(2):
                            sp.wait_ge(a_ql, 2 * it + u + 1)
                            for part, src in ((0, qh), (1, qh), (2, ql)):
                                sp.dma_start(q_d[:, :, part, bass.ds((2 * it + u) * 4 * P, 4 * P)],
                                             src[u][:, :]).then_inc(a_qd[u], 16)
                    sp.wait_ge(a_out, 48)
                    sp.wait_ge(a_kl, 16 * (G + 1))
                    for u in range(2):
                        sp.wait_ge(a_qd[u], 16 * PARTS * (NT // 8))

                @block.gpsimd
                def _(pool):
                    pool.memset(ident[:, :], 0.0).then_inc(a_id, 1)
                    pool.memset(sel3[:, :, :], 1.0).then_inc(a_id, 1)
                    pool.wait_ge(a_id, 2)
                    pool.affine_select(out=ident[:, :], in_=ident[:, :], compare_op=ALU.not_equal, fill=1.0,
                                       base=0, pattern=[[-1, P]], channel_multiplier=1).then_inc(a_id, 1)
                    pool.affine_select(out=sel3[:, :, :], in_=sel3[:, :, :], compare_op=ALU.is_ge, fill=0.0,
                                       base=0, pattern=[[-DH, GH], [-GD, G]], channel_multiplier=1).then_inc(a_pool, 1)
                    pool.wait_ge(a_pool, 1)
                    pool.affine_select(out=sel3[:, :, :], in_=sel3[:, :, :], compare_op=ALU.is_ge, fill=0.0,
                                       base=DH - 1, pattern=[[DH, GH], [GD, G]], channel_multiplier=-1).then_inc(a_pool, 1)
                    pool.wait_ge(a_pool, 2)
                    n = 0
                    for i in range(4):
                        for part, value in ((QS[i][0:96, :, :, :, :], 0.0), (QS[i][96:98, :, :, :, :], 1.0),
                                            (KS[i][96:98, :, :, :], 1.0), (VX[i][:, :, :, 1, :, GD:CW], 0.0)):
                            pool.memset(part, value).then_inc(a_fill, 1)
                            n += 1
                            pool.wait_ge(a_fill, n)

                @block.scalar
                def _(act):
                    act.wait_ge(a_pe, 1)
                    act.wait_ge(a_w, WD)
                    act.activation(klh[:, :], bank[1][:, 0:B], ACT.Identity, bias=bk_c[:, 0:1]).then_inc(a_klh, 1)

                    def block_of_queries(it, u):
                        act.wait_ge(a_xT, 2 * it + u + 1)
                        act.activation(xnT[u][:, :], bank[2 + u][:, :], ACT.Copy).then_inc(a_xTc, 1)
                        act.wait_ge(a_q32, 2 * it + u + 1)
                        wait(act, a_qd[u], 16 * PARTS * it)
                        act.activation(batch_last(qh[u]), batch_first(q32[u]), ACT.Copy).then_inc(a_qh, 1)

                    for u in range(2):
                        block_of_queries(0, u)
                    with act.Fori(1, NT // 8) as it:
                        for u in range(2):
                            block_of_queries(it, u)

                @block.vector
                def _(dve):
                    dve.wait_ge(a_w, WD)
                    dve.tensor_scalar(bias16[:, 0:KM].rearrange("b (c i) -> b i c", c=KC),
                                      mask_i[:, 0:KM].rearrange("b (i c) -> b i c", c=KC), 0.0, MASKED,
                                      ALU.is_equal, ALU.mult).then_inc(a_dve, 1)
                    dve.tensor_scalar(bias16[:, KM:SK], mask_i[:, KM:SK], 0.0, MASKED, ALU.is_equal, ALU.mult).then_inc(a_dve, 1)
                    dve.tensor_scalar(m01[:, :], mask_i[:, :], 0.0, None, ALU.not_equal).then_inc(a_dve, 1)
                    dve.tensor_copy(bvR[:, :], bv_c[:, 0:1].broadcast_to((P, D))).then_inc(a_dve, 1)
                    dve.wait_ge(a_wt, 1)
                    for k, w in enumerate((WqT, WkT, WvT, WoT)):
                        dve.tensor_copy(w[:, :], bank[0][:, k * D:(k + 1) * D]).then_inc(a_wtc, 1)
                    dve.wait_ge(a_wt, 2)
                    dve.tensor_copy(clT[:, :], bank[1][:, 0:P]).then_inc(a_wtc, 1)
                    dve.tensor_copy(maskT[:, :, :], bank[1][:, P:P + KC * B].rearrange("p (c b) -> p c b", c=KC)).then_inc(a_wtc, 1)
                    dve.wait_ge(a_pool, 2)
                    dve.tensor_reduce(rowsel[:, :], sel3[:, :, :], AX.X, ALU.max).then_inc(a_wtc, 1)
                    dve.wait_ge(a_wtc, 7)
                    for j in range(GH):
                        dve.tensor_scalar(WoM[:, j, :], WoT[:, :], rowsel[:, j:j + 1], None, ALU.mult).then_inc(a_wtc, 1)
                    dve.wait_ge(a_klh, 1)
                    dve.scalar_tensor_tensor(kll[:, :], bank[1][:, 0:B], bk_c[:, 0:1], klh[:, :],
                                             ALU.add, ALU.subtract).then_inc(a_last, 2)
                    dve.wait_ge(a_pe, 3)
                    dve.tensor_copy(vlast[:, :, 0:GD], bank[5][:, 0:D].rearrange("p (g c) -> p g c", g=G)).then_inc(a_last, 1)
                    dve.tensor_copy(vlast[:, :, GD:CW], m01[:, KM:SK].unsqueeze(1).broadcast_to((P, G, 1))).then_inc(a_last, 1)
                    dve.wait_ge(a_x, 16)
                    for t in range(NT):
                        dve.bn_stats(stats[:, t, :], xs[:, t, :]).then_inc(a_st, 1)
                    for t in range(NT):
                        dve.wait_ge(a_st, t + 1)
                        dve.bn_aggr(mv[:, t, :], stats[:, t, :]).then_inc(a_ag, 1)
                    dve.wait_ge(a_ag, NT)
                    inverse_deviation(dve, rstd[:, :], nwt[:, :], nw2[:, :], mv[:, :, 1], a_rs, 0)

                    def block_of_queries(it, u, first):
                        if not first:
                            dve.wait_ge(a_xT, 2 * it + u - 1)
                        for k in range(4):
                            t = (2 * it + u) * 4 + k
                            dve.tensor_scalar(xn[u][:, k, :], xs[:, bass.ds(t, 1), :], mv[:, bass.ds(t, 1), 0],
                                              rstd[:, bass.ds(t, 1)], ALU.subtract, ALU.mult).then_inc(a_xn, 1)
                        dve.wait_ge(a_q, 2 * it + u + 1)
                        dve.tensor_scalar(q32[u][:, :], bank[4 + u][:, :], bq_c[:, 0:1], SCALE,
                                          ALU.add, ALU.mult).then_inc(a_q32, 1)
                        dve.wait_ge(a_qh, 2 * it + u + 1)
                        wait(dve, a_qd[u], 16 * PARTS * it)
                        dve.tensor_tensor(batch_last(ql[u]), batch_first(q32[u]), batch_last(qh[u]), ALU.subtract).then_inc(a_ql, 1)

                    for u in range(2):
                        block_of_queries(0, u, True)
                    with dve.Fori(1, NT // 8) as it:
                        for u in range(2):
                            block_of_queries(it, u, False)
                    dve.wait_ge(a_pe, 2)
                    dve.tensor_tensor(boR[:, :], boR[:, :], bank[6][:, 0:D], ALU.add).then_inc(a_rs, 1)
                    dve.wait_ge(a_rs, 13)
                    for t in range(NT):
                        dve.tensor_tensor(xs[:, t, :], xs[:, t, :], boR[:, :], ALU.add)

                @block.tensor
                def _(pe):
                    pe.wait_ge(a_w, WD)
                    pe.wait_ge(a_id, 3)
                    for k in range(4):
                        last = pe.transpose(bank[0][:, k * D:(k + 1) * D], w_nat[:, k, :], ident[:, :])
                    last.then_inc(a_wt, 1)
                    pe.wait_ge(a_dve, 4)
                    pe.transpose(bank[1][:, 0:P], clast[:, :], ident[:, :])
                    for c in range(KC):
                        last = pe.transpose(bank[1][:, P + c * B:P + (c + 1) * B], m01[:, c:KM:KC], ident[:, :])
                    last.then_inc(a_wt, 1)
                    pe.wait_ge(a_wtc, 6)
                    pe.matmul(bank[1][:, 0:B], WkT[:, :], clT[:, :], start=True, stop=True).then_inc(a_pe, 1)
                    pe.matmul(bank[6][:, 0:D], bvR[:, :], WoT[:, :], start=True, stop=True).then_inc(a_pe, 1)
                    pe.matmul(bank[5][:, 0:D], clT[:, :], WvT[:, :], start=True, stop=True).then_inc(a_pe, 1)
                    pe.wait_ge(a_last, 3)

                    def block_of_queries(it, u, first):
                        for k in range(4):
                            pe.wait_ge(a_xn, (2 * it + u) * 4 + k + 1)
                            last = pe.transpose(bank[2 + u][:, k * P:(k + 1) * P], xn[u][:, k, :], ident[:, :])
                        last.then_inc(a_xT, 1)
                        pe.wait_ge(a_xTc, 2 * it + u + 1)
                        if not first:
                            pe.wait_ge(a_q32, 2 * it + u - 1)
                        pe.matmul(bank[4 + u][:, :], WqT[:, :], xnT[u][:, :], start=True, stop=True).then_inc(a_q, 1)

                    for u in range(2):
                        block_of_queries(0, u, True)
                    with pe.Fori(1, NT // 8) as it:
                        for u in range(2):
                            block_of_queries(it, u, False)

        with ExitStack() as S:
            cx = [sb(S, f"cx{i}", [P, PB, KC, D], F32) for i in range(2)]
            cT = [sb(S, f"cT{i}", [P, 2 * KM], F32) for i in range(2)]
            kh = [sb(S, f"kh{i}", [P, PB, KM], F16) for i in range(2)]
            kl = [sb(S, f"kl{i}", [P, PB, KM], F16) for i in range(2)]
            p32 = [sb(S, f"p32_{i}", [P, KC, 512], F32) for i in range(2)]
            ph = [sb(S, f"ph{i}", [P, KC, 512], F16) for i in range(4)]
            pl = [sb(S, f"pl{i}", [P, KC, 512], F16) for i in range(4)]
            mx = [sb(S, f"mx{i}", [P, G, PB], F32) for i in range(2)]
            KLP = [sb(S, f"KLP{i}", [P, G, PB], F16) for i in range(2)]
            nm16 = [sb(S, f"nm16_{i}", [P, G, PB], F16) for i in range(2)]
            sl = [sb(S, f"sl{i}", [P, G, PB], F32) for i in range(2)]
            plast = [sb(S, f"plast{i}", [P, G, PB], F32) for i in range(2)]
            tl = [sb(S, f"tl{i}", [P, PB, G, CW], F32) for i in range(2)]
            osum = [sb(S, f"osum{i}", [P, 2, G, CW], F32) for i in range(2)]
            orec = [sb(S, f"orec{i}", [P, 2, G], F32) for i in range(2)]
            on = [sb(S, f"on{i}", [P, 2, G, GD], F32) for i in range(2)]
            oT = sb(S, "oT", [P, GH, PB, SQ], F32)

            cxl = [sem(f"cxl{i}") for i in range(2)]
            ksl = [sem(f"ksl{i}") for i in range(4)]
            ksw = [sem(f"ksw{i}") for i in range(2)]
            qsl = [sem(f"qsl{i}") for i in range(4)]
            mrl = [sem(f"mrl{i}") for i in range(4)]
            vll = [sem(f"vll{i}") for i in range(4)]
            KSN, QSN, MRN = 16 * 2, 16 * GH, 16 * G
            tb_ready, tb_read = sem("tb_ready"), sem("tb_read")
            kb_ready, kh_done, kl_done = sem("kb_ready"), sem("kh_done"), sem("kl_done")
            vb_ready, vh_done, vl_done = sem("vb_ready"), sem("vh_done"), sem("vl_done")
            vm_done, kp_done = sem("vm_done"), sem("kp_done")
            r_ready, r_read = [sem("r_ready0"), sem("r_ready1")], [sem("r_read0"), sem("r_read1")]
            sl_ready, m_step, plast_done = sem("sl_ready"), sem("m_step"), sem("plast_done")
            t_ready, t_read = [sem("t_ready0"), sem("t_ready1")], [sem("t_read0"), sem("t_read1")]
            ph_done, pl_done, pv_done = sem("ph_done"), sem("pl_done"), sem("pv_done")
            tl_done, o_step = sem("tl_done"), sem("o_step")
            ot_ready, ot_read, y_ready, y_read = sem("ot_ready"), sem("ot_read"), sem("y_ready"), sem("y_read")

            RB, TBK, WB, OB, MB = bank[0:2], bank[2:4], bank[4:6], bank[6], bank[7]
            LB = OB[:, 2 * G * CW:2 * G * CW + G * PB]
            last_scores = LB.rearrange("p (g b) -> p g b", g=G)
            YB = MB[:, 0:D]
            MSTEPS, OSTEPS = 3, 3
            ND = 3
            NR = 2

            class Pack:
                def __init__(self, it, c):
                    self.it, self.c = it, c
                    self.n, self.m2, self.m4 = 4 * it + c, c % 2, c % 4
                    self.d2, self.d4 = 2 * it + c // 2, it + c // 4

                def plus(self, k):
                    return Pack(self.it, self.c + k)

                def after(self, k):
                    return self.c >= k

            def steps(eng, step):
                def peeled(s):
                    pk = lambda n: Pack(0, n) if 0 <= n < NPACK else None
                    step(pk(s), pk(s + NR), pk(s + ND), pk(s - 1), pk(s + 1), pk(s + ND + 1))
                for s in range(-ND - 1, 1):
                    peeled(s)
                full = (NPACK - ND - 4) // 4
                with eng.Fori(0, full) as it:
                    for k in range(4):
                        step(*(Pack(it, 1 + k + d) for d in (0, NR, ND, -1, 1, ND + 1)))
                for s in range(1 + 4 * full, NPACK + 1):
                    peeled(s)

            with nc.Block() as block:
                @block.sync
                def _(sp):
                    def load_ctx(p):
                        if p.after(2):
                            sp.wait_ge(tb_ready, 2 * p.n - 2)
                        sp.dma_start(cx[p.m2][:, :, :, :].rearrange("p b c d -> p b (c d)"),
                                     ctx[bass.ds(PB * p.n, PB), 0:KM, :].rearrange("b (p c) d -> p b (c d)", c=KC)
                                     ).then_inc(cxl[p.m2], 16)

                    def step(a, r, p, prev, nxt, q):
                        if p:
                            if p.after(4):
                                sp.wait_ge(t_ready[1], PB * (p.n - 3))
                                sp.wait_ge(tl_done, p.n - 3)
                            for j in range(GH):
                                rows = DH * PARTS
                                sp.dma_start(QS[p.m4][rows * j:rows * (j + 1), :, j, :, :].rearrange("i g q b -> i g (q b)"),
                                             q_d[:, DH * j:DH * (j + 1), :, bass.ds(P * p.n, P)]
                                             .rearrange("g d s q -> (d s) g q")).then_inc(qsl[p.m4], 16)
                            sp.dma_start(KS[p.m4][NROW:KROW, :, :, :].rearrange("o g b k -> o g (b k)"),
                                         bias_d[bass.ds(PB * p.n, PB), :].rearrange("b (o k) -> o (b k)", o=1)
                                         .unsqueeze(1).broadcast_to((1, G, PB * KM))).then_inc(ksl[p.m4], 16)
                            sp.dma_start(VL[p.m4][:, :, :, :].rearrange("p b g c -> p (b g c)"),
                                         vlast_d[bass.ds(PB * p.n, PB), :].rearrange("b (a n) -> a (b n)", a=1)
                                         .broadcast_to((P, PB * G * CW))).then_inc(vll[p.m4], 16)
                        if nxt:
                            sp.wait_ge(m_step, MSTEPS * nxt.n + 2)
                            for g in range(G):
                                sp.dma_start(QS[nxt.m4][SROW - 1:SROW, g, :, :, :].rearrange("o h q b -> o (h q b)"),
                                             nm16[nxt.m2][:, g, :]).then_inc(mrl[nxt.m4], 16)
                        if p:
                            sp.wait_ge(kl_done, 2 * p.n + 2)
                            sp.wait_ge(kh_done, 2 * p.n + 2)
                            for part, src in ((0, kh), (1, kl), (2, kh)):
                                sp.dma_start(k_d[p.m2, :, part, :, :].rearrange("i g n -> g i n"),
                                             src[p.m2][:, :, :].rearrange("p b k -> p (b k)")).then_inc(ksw[p.m2], 16)
                            sp.wait_ge(ksw[p.m2], 16 * PARTS * (p.d2 + 1))
                            sp.dma_start(KS[p.m4][0:NROW, :, :, :].rearrange("r g b k -> r (g b k)"),
                                         k_d[p.m2].rearrange("i s g n -> (i s) (g n)")).then_inc(ksl[p.m4], 16)
                            if not isinstance(p.n, int) or p.n + 2 < NPACK:
                                load_ctx(p.plus(2))

                    load_ctx(Pack(0, 0))
                    load_ctx(Pack(0, 1))
                    steps(sp, step)

                @block.gpsimd
                def _(pool):
                    def step(a, r, p, prev, nxt, q):
                        if r:
                            wait(pool, sl_ready, r.n - 1)
                            pool.tensor_copy(KLP[r.m2][0:KROW, :, :], KL[0:KROW, :, bass.ds(PB * r.n, PB)]).then_inc(kp_done, 1)
                        for j in range(PB if a else 0):
                            n = PB * a.n + j
                            pool.wait_ge(ph_done, n + 1)
                            if a.after(1):
                                pool.wait_ge(pv_done, n - 3)
                            pool.tensor_tensor(pl[j][:, :, :], p32[j % 2][:, :, :], ph[j][:, :, :],
                                               ALU.subtract).then_inc(pl_done, 1)
                            if j == 1:
                                pool.wait_ge(vll[a.m4], 16 * (a.d4 + 1))
                                pool.wait_ge(plast_done, a.n + 1)
                                if a.after(2):
                                    pool.wait_ge(o_step, OSTEPS * 2 * (a.n - 1))
                                for b in range(PB):
                                    last = pool.tensor_tensor(tl[a.m2][:, b, :, :], VL[a.m4][:, b, :, :],
                                                              plast[a.m2][:, :, b:b + 1].broadcast_to((P, G, CW)), ALU.mult)
                                last.then_inc(tl_done, 1)
                        if p:
                            if p.after(4):
                                pool.wait_ge(pv_done, PB * (p.n - 3))
                            pool.tensor_copy(VX[p.m4][:, :, :, 0, :, GD],
                                             maskT[:, :, bass.ds(PB * p.n, PB)].rearrange("p c b -> p b c")
                                             .unsqueeze(3).broadcast_to((P, PB, KC, G))).then_inc(vm_done, 1)
                    steps(pool, step)

                @block.scalar
                def _(act):
                    def exps(a, j):
                        n = PB * a.n + j
                        if a.after(1) or j >= 2:
                            act.wait_ge(pl_done, n - 1)
                        if a.after(1):
                            act.wait_ge(pv_done, n - 3)
                        act.wait_ge(t_ready[0], n + 1)
                        act.activation(p32[j % 2][:, 0, :], TBK[0][:, :], ACT.Exp)
                        act.activation(ph[j][:, 0, :], TBK[0][:, :], ACT.Exp).then_inc(t_read[0], 1)
                        act.wait_ge(t_ready[1], n + 1)
                        act.activation(p32[j % 2][:, 1, :], TBK[1][:, :], ACT.Exp).then_inc(t_read[1], 1)

                    def keys(p, u):
                        act.wait_ge(kb_ready, 2 * p.n + u + 1)
                        if u == 0 and (p.after(2)):
                            act.wait_ge(ksw[p.m2], 16 * PARTS * p.d2)
                        act.activation(kh[p.m2][:, 2 * u:2 * u + 2, :], WB[1 - u][:, :].rearrange("p (b k) -> p b k", b=2),
                                       ACT.Identity, bias=bk_c[:, 0:1]).then_inc(kh_done, 1)

                    def values(p, u):
                        act.wait_ge(vb_ready, 2 * p.n + u + 1)
                        if u == 0 and (p.after(4)):
                            act.wait_ge(pv_done, PB * (p.n - 3))
                        act.activation(VX[p.m4][:, 2 * u:2 * u + 2, :, 0, :, 0:GD].rearrange("p b c g d -> p (b c) g d"),
                                       WB[u][:, :].rearrange("p (x g d) -> p x g d", x=2 * KC, g=G),
                                       ACT.Copy).then_inc(vh_done, 1)

                    def context(p, u):
                        q = 2 * p.n + u
                        act.wait_ge(tb_ready, q + 1)
                        if p.after(1):
                            act.wait_ge(vb_ready, q - 1)
                        act.activation(cT[u][:, :], WB[u][:, :], ACT.Copy).then_inc(tb_read, 1)

                    def gather_o(pk, u):
                        act.wait_ge(ot_ready, 2 * pk.n + u + 1)
                        if u == 0 and (pk.after(1)):
                            act.wait_ge(y_ready, pk.n)
                        act.activation(oT[:, :, 2 * u:2 * u + 2, :].rearrange("p h b q -> p b h q"),
                                       MB[:, 0:256].rearrange("p (b h q) -> p b h q", b=2, h=GH),
                                       ACT.Copy).then_inc(ot_read, 1)

                    def step(a, r, p, prev, nxt, q):
                        for j in range(PB):
                            if a:
                                exps(a, j)
                            if j % 2 == 0 and p:
                                keys(p, j // 2)
                            if j % 2 == 0 and prev:
                                gather_o(prev, j // 2)
                            if j == 1 and p:
                                context(p, 1)
                            if j % 2 == 1 and p:
                                values(p, j // 2)
                            if j == 3 and q:
                                context(q, 0)
                            if j == 2 and nxt:
                                act.wait_ge(m_step, MSTEPS * (nxt.n + 1))
                                if nxt.after(2):
                                    act.wait_ge(tl_done, nxt.n - 1)
                                act.activation(plast[nxt.m2][:, :, :], sl[nxt.m2][:, :, :], ACT.Exp).then_inc(plast_done, 1)
                    steps(act, step)

                @block.vector
                def _(dve):
                    def maxima(r, j):
                        for hf in range(2):
                            dve.wait_ge(r_ready[hf], PB * r.n + j + 1)
                            dve.tensor_reduce(mx[r.m2][:, 2 * hf:2 * hf + 2, j], RB[hf][:, :].rearrange("p (g k) -> p g k", g=2),
                                              AX.X, ALU.max).then_inc(r_read[hf], 1)

                    def join_last_key(r):
                        dve.wait_ge(sl_ready, r.n + 1)
                        if r.after(2):
                            dve.wait_ge(pv_done, PB * r.plus(-1).n)
                        dve.wait_ge(r_read[1], PB * r.n + PB)
                        dve.tensor_tensor(mx[r.m2][:, :, :], last_scores, mx[r.m2][:, :, :], ALU.max).then_inc(m_step, 1)

                    def negate_maxima(r):
                        dve.wait_ge(m_step, MSTEPS * r.n + 1)
                        if r.after(2):
                            dve.wait_ge(mrl[r.plus(-2).m4], MRN * (r.plus(-2).d4 + 1))
                        dve.tensor_scalar(nm16[r.m2][:, :, :], mx[r.m2][:, :, :], -1.0, None, ALU.mult).then_inc(m_step, 1)

                    def shift_last_key(r):
                        dve.wait_ge(m_step, MSTEPS * r.n + 2)
                        if r.after(2):
                            dve.wait_ge(plast_done, r.n - 1)
                        dve.tensor_tensor(sl[r.m2][:, :, :], last_scores, nm16[r.m2][:, :, :], ALU.add).then_inc(m_step, 1)

                    def low_keys(p, u):
                        dve.wait_ge(kh_done, 2 * p.n + u + 1)
                        dve.scalar_tensor_tensor(kl[p.m2][:, 2 * u:2 * u + 2, :].rearrange("p b k -> p (b k)"),
                                                 WB[1 - u][:, :], bk_c[:, 0:1],
                                                 kh[p.m2][:, 2 * u:2 * u + 2, :].rearrange("p b k -> p (b k)"),
                                                 ALU.add, ALU.subtract).then_inc(kl_done, 1)

                    def low_values(p, u):
                        dve.wait_ge(vh_done, 2 * p.n + u + 1)
                        v = VX[p.m4][:, 2 * u:2 * u + 2, :, :, :, 0:GD].rearrange("p b c s g d -> p (b c) s g d")
                        dve.tensor_tensor(v[:, :, 1], WB[u][:, :].rearrange("p (x g d) -> p x g d", x=2 * KC, g=G),
                                          v[:, :, 0], ALU.subtract).then_inc(vl_done, 1)

                    def high_part(a, j):
                        dve.wait_ge(t_read[1], PB * a.n + j + 1)
                        dve.tensor_copy(ph[j][:, 1, :], p32[j % 2][:, 1, :]).then_inc(ph_done, 1)

                    def sums(pk, u):
                        dve.wait_ge(pv_done, PB * pk.n + 2 * u + 2)
                        dve.wait_ge(tl_done, pk.n + 1)
                        dve.tensor_tensor(osum[u][:, :, :, :], OB[:, 0:2 * G * CW].rearrange("p (b g c) -> p b g c", b=2, g=G),
                                          tl[pk.m2][:, 2 * u:2 * u + 2, :, :], ALU.add).then_inc(o_step, 1)

                    def reciprocals(pk, u):
                        dve.wait_ge(o_step, OSTEPS * (2 * pk.n + u) + 1)
                        dve.reciprocal(orec[u][:, :, :], osum[u][:, :, :, GD]).then_inc(o_step, 1)

                    def quotients(pk, u):
                        dve.wait_ge(o_step, OSTEPS * (2 * pk.n + u) + 2)
                        if pk.after(1):
                            dve.wait_ge(ot_ready, 2 * pk.n + u - 1)
                        dve.tensor_tensor(on[u][:, :, :, :], osum[u][:, :, :, 0:GD],
                                          orec[u][:, :, :].unsqueeze(3).broadcast_to((P, 2, G, GD)),
                                          ALU.mult).then_inc(o_step, 1)

                    def step(a, r, p, prev, nxt, q):
                        for j in range(PB):
                            if j < 2 and nxt:
                                maxima(nxt, j + 2)
                            if j >= 2 and r:
                                maxima(r, j - 2)
                            pk, u = {1: (prev, 1), 3: (a, 0)}.get(j, (None, 0))
                            if j == 1 and nxt:
                                join_last_key(nxt)
                            if a and j == 1:
                                high_part(a, j)
                            if pk:
                                sums(pk, u)
                            if j == 1 and nxt:
                                negate_maxima(nxt)
                            if pk:
                                reciprocals(pk, u)
                            if j == 1 and nxt:
                                shift_last_key(nxt)
                            if a and j != 1:
                                high_part(a, j)
                            if pk:
                                quotients(pk, u)
                            if j % 2 == 0 and p:
                                low_keys(p, j // 2)
                            if j % 2 == 1 and p:
                                low_values(p, j // 2)
                            if j == 3 and prev:
                                dve.wait_ge(y_ready, prev.n + 1)
                                dve.tensor_tensor(xs[:, bass.ds(prev.n, 1), :], YB.unsqueeze(1),
                                                  xs[:, bass.ds(prev.n, 1), :], ALU.add).then_inc(y_read, 1)
                    steps(dve, step)

                @block.tensor
                def _(pe):
                    def transposed_context(p, u):
                        q = 2 * p.n + u
                        if u == 0:
                            pe.wait_ge(cxl[p.m2], 16 * (p.d2 + 1))
                        wait(pe, kl_done, q)
                        for k in range(2 * KC):
                            last = pe.transpose(WB[u][:, k * P:(k + 1) * P], cx[p.m2][:, 2 * u + k // KC, k % KC, :], ident[:, :])
                        last.then_inc(tb_ready, 1)

                    def project(p, u):
                        q = 2 * p.n + u
                        pe.wait_ge(tb_read, q + 1)
                        wait(pe, vl_done, q)
                        pe.matmul(WB[1 - u][:, :], WkT[:, :], cT[u][:, :], start=True, stop=True).then_inc(kb_ready, 1)
                        for k in range(2 * KC):
                            last = pe.matmul(WB[u][:, k * D:(k + 1) * D], cT[u][:, k * P:(k + 1) * P], WvT[:, :],
                                             start=True, stop=True)
                        last.then_inc(vb_ready, 1)

                    def queries(pk, g, b, rows):
                        return QS[pk.m4][0:rows, g, :, :, b].rearrange("k h q -> k (h q)")

                    def row_scores(r, j):
                        if j == 0:
                            pe.wait_ge(ksl[r.m4], KSN * (r.d4 + 1))
                            pe.wait_ge(qsl[r.m4], QSN * (r.d4 + 1))
                        for hf in range(2):
                            wait(pe, r_read[hf], PB * r.n + j)
                            for g in (2 * hf, 2 * hf + 1):
                                last = pe.matmul(RB[hf][:, (g % 2) * KM:(g % 2 + 1) * KM], queries(r, g, j, KROW),
                                                 KS[r.m4][0:KROW, g, j, :], start=True, stop=True)
                            last.then_inc(r_ready[hf], 1)

                    def last_key_scores(r):
                        pe.wait_ge(kp_done, r.n + 1)
                        wait(pe, m_step, MSTEPS * r.n)
                        if r.after(2):
                            pe.wait_ge(o_step, OSTEPS * 2 * r.plus(-2).n + 1)
                        for g in range(G):
                            for b in range(PB):
                                last = pe.matmul(LB[:, g * PB + b:g * PB + b + 1], queries(r, g, b, KROW),
                                                 KLP[r.m2][0:KROW, g, b:b + 1], start=True, stop=True)
                        last.then_inc(sl_ready, 1)

                    def scores(a, j):
                        if j == 0:
                            pe.wait_ge(mrl[a.m4], MRN * (a.d4 + 1))
                        for c in range(KC):
                            wait(pe, t_read[c], PB * a.n + j)
                            for g in range(G):
                                last = pe.matmul(TBK[c][:, g * P:(g + 1) * P], KS[a.m4][0:SROW, g, j, c * P:(c + 1) * P],
                                                 queries(a, g, j, SROW), start=True, stop=True)
                            last.then_inc(t_ready[c], 1)

                    def outputs(pk, j):
                        n = PB * pk.n + j
                        pe.wait_ge(pl_done, n + 1)
                        if j == 0:
                            pe.wait_ge(vl_done, 2 * pk.n + 2)
                            pe.wait_ge(vm_done, pk.n + 1)
                        if j % 2 == 0:
                            m = 2 * pk.n + j // 2
                            if pk.after(1) or j:
                                pe.wait_ge(o_step, OSTEPS * m - 2)
                        for g in range(G):
                            o = OB[:, (j % 2 * G + g) * CW:(j % 2 * G + g + 1) * CW]
                            for c in range(KC):
                                v = VX[pk.m4][:, j, c, :, g, :]
                                hi, lo = (s[j][:, c, g * P:(g + 1) * P] for s in (ph, pl))
                                pe.matmul(o, hi, v[:, 0, :], start=(c == 0), stop=False)
                                pe.matmul(o, hi, v[:, 1, :], start=False, stop=False)
                                last = pe.matmul(o, lo, v[:, 0, :], start=False, stop=(c == KC - 1))
                        last.then_inc(pv_done, 1)

                    def transposed_outputs(pk, u):
                        pe.wait_ge(o_step, OSTEPS * (2 * pk.n + u + 1))
                        wait(pe, *((y_read, pk.n), (ot_read, 2 * pk.n + 1))[u])
                        for b in range(2):
                            last = pe.transpose(MB[:, b * P:(b + 1) * P], on[u][:, b, :, :].rearrange("p g d -> p (g d)"), ident[:, :])
                        last.then_inc(ot_ready, 1)

                    def step(a, r, p, prev, nxt, q):
                        for j in range(PB):
                            if a:
                                scores(a, j)
                            if j < 2 and nxt:
                                row_scores(nxt, j + 2)
                            if j >= 2 and r:
                                row_scores(r, j - 2)
                            if j == 0 and nxt:
                                last_key_scores(nxt)
                            if j == 1 and p:
                                transposed_context(p, 1)
                            if j == 3 and q:
                                transposed_context(q, 0)
                            if j < 2 and prev:
                                outputs(prev, j + 2)
                            if j >= 2 and a:
                                if j == 2 and nxt:
                                    pe.wait_ge(m_step, MSTEPS * (nxt.n + 1))
                                outputs(a, j - 2)
                            if j % 2 == 0 and p:
                                project(p, j // 2)
                            if j % 2 == 0 and prev:
                                transposed_outputs(prev, j // 2)
                            if j == 3 and prev:
                                pe.wait_ge(ot_read, 2 * prev.n + 2)
                                for h in range(GH):
                                    last = pe.matmul(YB[:, :], oT[:, h, :, :].rearrange("p b q -> p (b q)"), WoM[:, h, :],
                                                     start=(h == 0), stop=(h == GH - 1))
                                last.then_inc(y_ready, 1)
                    steps(pe, step)

        cross.close()

        with ExitStack() as S:
            E3 = 3 * D
            NB4 = 4 * PB
            NBLK = NT // 4
            Wqkv = sb(S, "Wqkv", [P, E3], F32)
            Wout = sb(S, "Wout", [P, D], F32)
            WoutM = sb(S, "WoutM", [P, GH, D], F32)
            bqk_c = sb(S, "bqk_c", [P, 2], F32)
            bv2_c = sb(S, "bv2_c", [P, 1], F32)
            bv2R = sb(S, "bv2R", [P, D], F32)
            boutR = sb(S, "boutR", [P, D], F32)
            st2 = sb(S, "st2", [P, 4, 6], F32)
            mv2 = sb(S, "mv2", [P, 4, 2], F32)
            turn2 = sb(S, "turn2", [P, 1], F32)
            rs2, rw2, rt2 = (sb(S, f"rs2_{i}", [P, 4], F32) for i in range(3))
            xm = sb(S, "xm", [P, 4, D], F32)
            xmT = sb(S, "xmT", [P, 4 * P], F32)
            qkh = [[sb(S, f"qkh{i}{k}", [P, 4 * P], F16) for k in range(2)] for i in range(2)]
            qkl = [[sb(S, f"qkl{i}{k}", [P, 4 * P], F16) for k in range(2)] for i in range(2)]
            vn = [sb(S, f"vn{i}", [P, 4, D], F32) for i in range(2)]
            Q2 = [sb(S, f"Q2_{i}", [NROW, G, GH, SQ, NB4], F16) for i in range(2)]
            K2 = [sb(S, f"K2_{i}", [NROW, G, 4 * P], F16) for i in range(2)]
            V2 = [sb(S, f"V2_{i}", [P, NB4, G, GD], F32) for i in range(2)]
            dif = [sb(S, f"dif{i}", [P, PB, G, SQ], F32) for i in range(2)]
            mx2 = [sb(S, f"mx2_{i}", [P, PB, G], F32) for i in range(2)]
            sm2 = [sb(S, f"sm2_{i}", [P, PB, G], F32) for i in range(4)]
            rc2 = [sb(S, f"rc2_{i}", [P, PB, G], F32) for i in range(4)]
            pr = [sb(S, f"pr{i}", [P, PB, G, SQ], F32) for i in range(4)]
            pT = [sb(S, f"pT{i}", [P, PB * P], F32) for i in range(2)]
            oT2 = [sb(S, f"oT2_{i}", [P, GH, PB, SQ], F32) for i in range(2)]

            q2_d = nc.dram_tensor("q2_parts_dram", [2, G, GD, PARTS, 4 * P], F16, kind="Internal").ap()
            k2_d = nc.dram_tensor("k2_parts_dram", [2, G, GD, PARTS, 4 * P], F16, kind="Internal").ap()
            v2_d = nc.dram_tensor("v2_dram", [2, NB4, SQ, D], F32, kind="Internal").ap()

            c_w, c_wm, c_pool, c_b, c_bias = sem("c_w"), sem("c_wm"), sem("c_pool"), sem("c_b"), sem("c_bias")
            c_ln, c_xm = sem("c_ln"), sem("c_xm")
            c_xT, c_xTc, c_pq, c_pv = sem("c_xT"), sem("c_xTc"), sem("c_pq"), sem("c_pv")
            c_hi, c_lo, c_vn = sem("c_hi"), sem("c_lo"), sem("c_vn")
            c_wr = [sem(f"c_wr{i}") for i in range(2)]
            c_vw = [sem(f"c_vw{i}") for i in range(2)]
            c_qk = [sem(f"c_qk{i}") for i in range(2)]
            c_v2 = [sem(f"c_v2{i}") for i in range(2)]
            c_s, c_mx, c_dif, c_exp, c_sum, c_rc, c_nrm = (sem("c_s"), sem("c_mx"), sem("c_dif"), sem("c_exp"),
                                                           sem("c_sum"), sem("c_rc"), sem("c_nrm"))
            c_tr, c_trc, c_o, c_oc, c_y, c_yr = (sem("c_tr"), sem("c_trc"), sem("c_o"), sem("c_oc"),
                                                 sem("c_y"), sem("c_yr"))
            WRN = 16 * 2 * PARTS

            class Step:
                def __init__(self, it, c):
                    self.it, self.c, self.s = it, c, 2 * it + c

                def block(self, k):
                    b = Tokens4(self.it, self.c + k)
                    return b if not isinstance(b.n, int) or 0 <= b.n < NBLK else None

                def tile(self, k):
                    n = 4 * self.s + k
                    return n if not isinstance(n, int) or 0 <= n < NT else None

            class Tokens4:
                def __init__(self, it, c):
                    self.n, self.m2, self.d2 = 2 * it + c, c % 2, it + c // 2

            def blocks(step):
                def run(eng):
                    for s in range(-2, 1):
                        step(Step(0, s))
                    full = (NBLK - 3) // 2
                    with eng.Fori(0, full) as it:
                        for k in range(2):
                            step(Step(it, 1 + k))
                    for s in range(1 + 2 * full, NBLK + 1):
                        step(Step(0, s))
                return run

            def side_by_side(st, w):
                return tuple(st.tile(w + k) for k in (2, 1, 0, -1, -2))

            with nc.Block() as block:
                @block.sync
                def _(sp):
                    sp.dma_start(Wqkv[:, :], W_qkv).then_inc(c_w, 16)
                    sp.dma_start(Wout[:, :], W_out).then_inc(c_w, 16)
                    for k in range(2):
                        sp.dma_start(bqk_c[:, k:k + 1], b_qkv[k * D:(k + 1) * D].rearrange("(p a) -> p a", a=1)).then_inc(c_w, 16)
                    sp.dma_start(bv2_c[:, :], b_qkv[2 * D:E3].rearrange("(p a) -> p a", a=1)).then_inc(c_w, 16)
                    sp.dma_start(boutR[:, :], b_out.rearrange("(a n) -> a n", a=1).broadcast_to((P, D))).then_inc(c_w, 16)
                    sp.wait_ge(c_pool, 4)

                    def step(st):
                        f = st.block(2)
                        v = st.block(1)
                        if v:
                            wait(sp, c_o, 4 * (v.n - 1))
                            sp.wait_ge(c_vw[v.m2], 16 * (v.d2 + 1))
                            for g in range(G):
                                sp.dma_start(V2[v.m2][SQ * g:SQ * (g + 1), :, g, :],
                                             v2_d[v.m2, :, :, GD * g:GD * (g + 1)].rearrange("b k c -> k b c")
                                             ).then_inc(c_v2[v.m2], 16)
                        if f:
                            for k, dram in enumerate((q2_d, k2_d)):
                                sp.wait_ge(c_lo, 2 * f.n + k + 1)
                                for part in range(PARTS):
                                    src = (qkh, qkh, qkl)[part] if k == 0 else (qkh, qkl, qkh)[part]
                                    sp.dma_start(dram[f.m2, :, :, part, :].rearrange("g i n -> (g i) n"), src[f.m2][k][:, :]).then_inc(c_wr[f.m2], 16)
                            sp.wait_ge(c_vn, f.n + 1)
                            sp.dma_start(v2_d[f.m2].rearrange("(t b) k c -> (b k) t c", t=4), vn[f.m2][:, :, :]).then_inc(c_vw[f.m2], 16)
                            sp.wait_ge(c_wr[f.m2], WRN * (f.d2 + 1))
                            wait(sp, c_s, 4 * f.n - 4)
                            for j in range(GH):
                                rows = DH * PARTS
                                sp.dma_start(Q2[f.m2][rows * j:rows * (j + 1), :, j, :, :].rearrange("i g q b -> i g (q b)"),
                                             q2_d[f.m2, :, DH * j:DH * (j + 1), :, :].rearrange("g d s q -> (d s) g q")
                                             ).then_inc(c_qk[f.m2], 16)
                            sp.dma_start(K2[f.m2][:, :, :], k2_d[f.m2].rearrange("g i s n -> (i s) g n")).then_inc(c_qk[f.m2], 16)
                    blocks(step)(sp)

                @block.gpsimd
                def _(pool):
                    for i in range(2):
                        for t in (Q2[i][:, :, :, :, :], V2[i][:, :, :, :]):
                            pool.memset(t, 0.0).then_inc(c_pool, 1)

                    def step(st):
                        f = st.block(2)
                        for w in range(4):
                            sc, nm, tr, pv, y = side_by_side(st, w)
                            if nm is not None:
                                i = (w + 1) % 4
                                pool.wait_ge(c_rc, 2 * nm + 2)
                                pool.tensor_tensor(pr[i][:, :, :, :], pr[i][:, :, :, :],
                                                   rc2[i][:, :, :].unsqueeze(3).broadcast_to((P, PB, G, SQ)),
                                                   ALU.mult).then_inc(c_nrm, 1)
                    pool.wait_ge(c_pool, 4)
                    blocks(step)(pool)

                def blocks_first(t):
                    return t.rearrange("p (b q) -> p q b", q=SQ)

                def blocks_last(t):
                    return t.rearrange("p (q b) -> p q b", q=SQ)

                @block.scalar
                def _(act):
                    def step(st):
                        f = st.block(2)
                        for w in range(4):
                            sc, nm, tr, pv, y = side_by_side(st, w)
                            if f and w == 0:
                                act.wait_ge(c_xT, f.n + 1)
                                act.activation(xmT[:, :], bank[0][:, :], ACT.Copy).then_inc(c_xTc, 1)
                            if f and w in (1, 2):
                                k = w - 1
                                act.wait_ge(c_pq, 2 * f.n + w)
                                wait(act, c_wr[f.m2], WRN * f.d2)
                                out = qkh[f.m2][k][:, :]
                                src = bank[1][:, :]
                                if k == 0:
                                    out, src = blocks_last(out), blocks_first(src)
                                act.activation(out, src, ACT.Identity, bias=bqk_c[:, k:k + 1]).then_inc(c_hi, 1)
                            if f and w == 3:
                                act.wait_ge(c_pv, f.n + 1)
                                wait(act, c_vw[f.m2], 16 * f.d2)
                                act.activation(vn[f.m2][:, :, :], bank[0][:, :].rearrange("p (t c) -> p t c", t=4),
                                               ACT.Copy).then_inc(c_vn, 1)
                            if tr is not None:
                                act.wait_ge(c_tr, tr + 1)
                                wait(act, c_o, tr - 1)
                                act.activation(pT[w % 2][:, :], bank[4 + w % 2][:, :], ACT.Copy).then_inc(c_trc, 1)
                            if pv is not None:
                                i = (w + 1) % 2
                                act.wait_ge(c_o, pv + 1)
                                wait(act, c_y, pv - 1)
                                act.activation(oT2[i][:, :, :, :].rearrange("p h b q -> p b h q"),
                                               bank[6][:, :].rearrange("p (b h q) -> p b h q", b=PB, h=GH),
                                               ACT.Copy).then_inc(c_oc, 1)
                            if sc is not None:
                                i = (w + 2) % 4
                                act.wait_ge(c_dif, sc + 1)
                                wait(act, c_tr, sc - 3)
                                act.activation(pr[i][:, :, :, :], dif[w % 2][:, :, :, :], ACT.Exp).then_inc(c_exp, 1)
                    blocks(step)(act)

                @block.vector
                def _(dve):
                    dve.wait_ge(c_w, 16 * 6)
                    dve.tensor_scalar(bv2R[:, :], bv2_c[:, 0:1].broadcast_to((P, D)), float(D) ** -0.5, None, ALU.mult).then_inc(c_wm, 1)
                    for j in range(GH):
                        dve.tensor_scalar(WoutM[:, j, :], Wout[:, :], rowsel[:, j:j + 1], None, ALU.mult).then_inc(c_wm, 1)
                    dve.wait_ge(c_b, 1)
                    dve.tensor_tensor(boutR[:, :], bank[7][:, 0:D], boutR[:, :], ALU.add).then_inc(c_wm, 1)

                    def step(st):
                        f = st.block(2)
                        for w in range(4):
                            sc, nm, tr, pv, y = side_by_side(st, w)
                            if sc is not None:
                                i = w % 2
                                sv = bank[2 + i][:, :].rearrange("p (b g k) -> p b g k", b=PB, g=G)
                                dve.wait_ge(c_s, sc + 1)
                                dve.tensor_reduce(mx2[i][:, :, :], sv, AX.X, ALU.max).then_inc(c_mx, 1)
                                dve.wait_ge(c_mx, sc + 1)
                                wait(dve, c_exp, sc - 1)
                                dve.tensor_tensor(dif[i][:, :, :, :], sv, mx2[i][:, :, :].unsqueeze(3).broadcast_to((P, PB, G, SQ)),
                                                  ALU.subtract).then_inc(c_dif, 1)
                            if f and w == 0:
                                base = 4 * f.n
                                ln = (8 + RSTD_STEPS) * f.n
                                for k in range(4):
                                    dve.bn_stats(st2[:, k, :], xs[:, bass.ds(base + k, 1), :].rearrange("p a c -> p (a c)")
                                                 ).then_inc(c_ln, 1)
                                dve.wait_ge(c_ln, ln + 4)
                                dve.memset(turn2[:, :], 0.0)
                                for k in range(4):
                                    dve.bn_aggr(mv2[:, k, :], st2[:, k, :]).then_inc(c_ln, 1)
                                dve.wait_ge(c_ln, ln + 8)
                                inverse_deviation(dve, rs2[:, :], rw2[:, :], rt2[:, :], mv2[:, :, 1], c_ln, ln + 8)
                                wait(dve, c_xT, f.n)
                                for k in range(4):
                                    dve.tensor_scalar(xm[:, k, :], xs[:, bass.ds(base + k, 1), :].rearrange("p a c -> p (a c)"),
                                                      mv2[:, k, 0:1], rs2[:, k:k + 1], ALU.subtract, ALU.mult).then_inc(c_xm, 1)
                                dve.wait_ge(c_wm, 6)
                                dve.wait_ge(c_xm, base + 4)
                                dve.tensor_tensor(xs[:, bass.ds(base, 4), :], xs[:, bass.ds(base, 4), :],
                                                  boutR[:, :].unsqueeze(1).broadcast_to((P, 4, D)), ALU.add).then_inc(c_bias, 1)
                            if f and w in (1, 2):
                                k = w - 1
                                hi, lo, src = qkh[f.m2][k][:, :], qkl[f.m2][k][:, :], bank[1][:, :]
                                if k == 0:
                                    hi, lo, src = blocks_last(hi), blocks_last(lo), blocks_first(src)
                                dve.wait_ge(c_hi, 2 * f.n + w)
                                dve.scalar_tensor_tensor(lo, src, bqk_c[:, k:k + 1], hi, ALU.add, ALU.subtract).then_inc(c_lo, 1)
                            if nm is not None:
                                i = (w + 1) % 4
                                dve.wait_ge(c_exp, nm + 1)
                                dve.tensor_reduce(sm2[i][:, :, :], pr[i][:, :, :, :], AX.X, ALU.add).then_inc(c_sum, 1)
                                dve.wait_ge(c_sum, nm + 1)
                                dve.reciprocal(rc2[i][:, :, :], sm2[i][:, :, :]).then_inc(c_rc, 1)
                                dve.wait_ge(c_rc, 2 * nm + 1)
                                dve.tensor_scalar(rc2[i][:, :, :], rc2[i][:, :, :], float(D) ** -0.5, None, ALU.mult).then_inc(c_rc, 1)
                            if y is not None:
                                dve.wait_ge(c_y, y + 1)
                                dve.wait_ge(c_bias, (st.block(0) if w >= 2 else st.block(-1)).n + 1)
                                dve.tensor_tensor(xs[:, bass.ds(y, 1), :], bank[7][:, 0:D].unsqueeze(1),
                                                  xs[:, bass.ds(y, 1), :], ALU.add).then_inc(c_yr, 1)
                    blocks(step)(dve)

                @block.tensor
                def _(pe):
                    pe.wait_ge(c_w, 16 * 6)
                    pe.wait_ge(c_wm, 1)
                    pe.matmul(bank[7][:, 0:D], bv2R[:, :], Wout[:, :], start=True, stop=True).then_inc(c_b, 1)
                    pe.wait_ge(c_wm, 6)

                    def step(st):
                        f = st.block(2)
                        for w in range(4):
                            sc, nm, tr, pv, y = side_by_side(st, w)
                            if sc is not None:
                                bl = st.block((w + 2) // 4)
                                m = bl.m2
                                if w == 2:
                                    pe.wait_ge(c_qk[m], 16 * (GH + 1) * (bl.d2 + 1))
                                wait(pe, c_dif, sc - 1)
                                t = (w + 2) % 4
                                for b in range(PB):
                                    for g in range(G):
                                        last = pe.matmul(bank[2 + w % 2][:, (b * G + g) * SQ:(b * G + g + 1) * SQ],
                                                         Q2[m][:, g, :, :, t * PB + b].rearrange("k h q -> k (h q)"),
                                                         K2[m][:, g, (t * PB + b) * SQ:(t * PB + b + 1) * SQ], start=True, stop=True)
                                last.then_inc(c_s, 1)
                            if f and w == 0:
                                wait(pe, c_vn, f.n)
                                pe.wait_ge(c_xm, 4 * f.n + 4)
                                for k in range(4):
                                    last = pe.transpose(bank[0][:, k * P:(k + 1) * P], xm[:, k, :], ident[:, :])
                                last.then_inc(c_xT, 1)
                            if f and w in (1, 2):
                                pe.wait_ge(c_xTc, f.n + 1)
                                wait(pe, c_lo, 2 * f.n + w - 1)
                                pe.matmul(bank[1][:, :], Wqkv[:, (w - 1) * D:w * D], xmT[:, :], start=True, stop=True).then_inc(c_pq, 1)
                            if f and w == 3:
                                for k in range(4):
                                    last = pe.matmul(bank[0][:, k * D:(k + 1) * D], xmT[:, k * P:(k + 1) * P], Wqkv[:, 2 * D:E3],
                                                     start=True, stop=True)
                                last.then_inc(c_pv, 1)
                            if tr is not None:
                                pe.wait_ge(c_nrm, tr + 1)
                                wait(pe, c_trc, tr - 1)
                                for b in range(PB):
                                    last = pe.transpose(bank[4 + w % 2][:, b * P:(b + 1) * P],
                                                        pr[w][:, b, :, :].rearrange("p g k -> p (g k)"), ident[:, :])
                                last.then_inc(c_tr, 1)
                            if pv is not None:
                                bl = st.block((w - 1) // 4)
                                m = bl.m2
                                if w == 1:
                                    pe.wait_ge(c_v2[m], 16 * G * (bl.d2 + 1))
                                pe.wait_ge(c_trc, pv + 1)
                                wait(pe, c_oc, pv)
                                t = (w - 1) % 4
                                for b in range(PB):
                                    last = pe.matmul(bank[6][:, b * P:(b + 1) * P],
                                                     V2[m][:, t * PB + b, :, :].rearrange("k g c -> k (g c)"),
                                                     pT[(w + 1) % 2][:, b * P:(b + 1) * P], start=True, stop=True)
                                last.then_inc(c_o, 1)
                            if y is not None:
                                pe.wait_ge(c_oc, y + 1)
                                wait(pe, c_yr, y)
                                for h in range(GH):
                                    last = pe.matmul(bank[7][:, 0:D], oT2[w % 2][:, h, :, :].rearrange("p b q -> p (b q)"),
                                                     WoutM[:, h, :], start=(h == 0), stop=(h == GH - 1))
                                last.then_inc(c_y, 1)
                    blocks(step)(pe)

        L, E, _, F = w1.shape
        FC = F // P
        LE = L * E
        NBLK = NT // 4
        NSTEP = L * NBLK
        WS = 64.0
        moe = whole.enter_context(ExitStack())
        hs = sb(moe, "hs", [P, NT, D], F32)
        w1p = sb(moe, "w1p", [P, 2, LE, F], F16)
        w2p = sb(moe, "w2p", [P, 2, LE, FC, D], F16)
        rwp = sb(moe, "rwp", [P, 2, L, E], F16)
        b2p = sb(moe, "b2p", [P, LE, D], F16)
        ones = sb(moe, "ones", [P, P], F16)
        b1c = sb(moe, "b1c", [P, LE, FC], F32)
        srw = sb(moe, "srw", [P, L, E], F32)
        rbR = sb(moe, "rbR", [P, L, E], F32)
        lower = sb(moe, "lower", [P, E, E], F32)

        with ExitStack() as S:
            w1f = sb(S, "w1f", [P, LE, F], F32)
            b2f = sb(S, "b2f", [P, LE * D], F32)
            rwf = sb(S, "rwf", [P, L, E], F32)
            ones32 = sb(S, "ones32", [P, P], F32)
            rows = sb(S, "rows", [P, P], F32)
            cols = sb(S, "cols", [P, P], F32)
            gain = sb(S, "gain", [P, LE], F32)
            b2t = sb(S, "b2t", [P, LE * D], F16)
            w2f = sb(S, "w2f", [P, 2, E * FC, D], F32)
            st3 = sb(S, "st3", [P, NT, 6], F32)
            mv3 = sb(S, "mv3", [P, NT, 2], F32)
            rs3, rw3, rt3 = (sb(S, f"rs3_{i}", [P, NT], F32) for i in range(3))
            e_row, e_small, e_fill = sem("e_row"), sem("e_small"), sem("e_fill")
            e_w1 = [sem(f"e_w1{l}") for l in range(L)]
            e_w2 = [sem(f"e_w2{l}") for l in range(2)]
            e_T, e_cols, e_gain, e_b1, e_srw = sem("e_T"), sem("e_cols"), sem("e_gain"), sem("e_b1"), sem("e_srw")
            e_h1, e_h2, e_l2, e_rwh, e_b2, e_ln = sem("e_h1"), sem("e_h2"), sem("e_l2"), sem("e_rwh"), sem("e_b2"), sem("e_ln")
            d_acc = sem("d_acc")

            with nc.Block() as block:
                @block.sync
                def _(sp):
                    sp.wait_ge(e_fill, 1)
                    sp.dma_start(rows[0:LE, :], ln_g.rearrange("l e h -> (l e) h")).then_inc(e_row, 16)
                    sp.dma_start(rows[32:32 + LE, :], ln_b.rearrange("l e h -> (l e) h")).then_inc(e_row, 16)
                    sp.dma_start(rows[64:64 + LE * FC, :], b1.rearrange("l e (c f) -> (l e c) f", f=P)).then_inc(e_row, 16)
                    sp.dma_start(rwf[:, :, :], router_w.rearrange("l h e -> h l e")).then_inc(e_small, 16)
                    sp.dma_start(rbR[:, :, :].rearrange("p l e -> p (l e)"),
                                 router_b.rearrange("(a l) e -> a (l e)", a=1).broadcast_to((P, LE))).then_inc(e_small, 16)
                    for r in (0, 32):
                        sp.dma_start(b2f[r:r + 1, :], b2.rearrange("(a l) e h -> a (l e h)", a=1)).then_inc(e_small, 16)
                    for l in range(L):
                        sp.dma_start(w1f[:, l * E:(l + 1) * E, :], w1[l].rearrange("e h f -> h e f")).then_inc(e_w1[l], 16)
                    for l in range(L):
                        if l >= 2:
                            sp.wait_ge(e_l2, l - 1)
                        sp.dma_start(w2f[:, l % 2, :, :], w2[l].rearrange("e (c f) h -> f (e c) h", f=P)).then_inc(e_w2[l % 2], 16)

                @block.gpsimd
                def _(pool):
                    pool.memset(rows[:, :], 0.0).then_inc(e_fill, 1)
                    pool.wait_ge(e_fill, 1)
                    pool.memset(ones32[:, :], 1.0).then_inc(e_fill, 1)
                    pool.memset(ones[:, :], 1.0).then_inc(e_fill, 1)
                    pool.memset(b2p[:, :, :], 0.0).then_inc(e_fill, 1)
                    pool.memset(lower[:, :, :], 0.0).then_inc(e_fill, 1)
                    pool.wait_ge(e_fill, 5)
                    for e in range(1, E):
                        pool.memset(lower[:, e, 0:e], 1.0).then_inc(e_fill, 1)

                @block.scalar
                def _(act):
                    act.wait_ge(e_small, 64)
                    act.activation(rwp[:, 0, :, :], rwf[:, :, :], ACT.Copy, scale=WS).then_inc(e_rwh, 1)
                    act.wait_ge(e_gain, 1)
                    for le in range(LE):
                        if le % E == 0:
                            act.wait_ge(e_w1[le // E], 16)
                        act.activation(w1p[:, 0, le, :], w1f[:, le, :], ACT.Copy, scale=gain[:, le:le + 1]).then_inc(e_h1, 1)
                    for l in range(L):
                        act.wait_ge(e_w2[l % 2], 16 * (l // 2 + 1))
                        act.activation(w2p[:, 0, l * E:(l + 1) * E, :, :].rearrange("p e c h -> p (e c) h"),
                                       w2f[:, l % 2, :, :], ACT.Copy, scale=WS).then_inc(e_h2, 1)

                @block.vector
                def _(dve):
                    for t in range(NT):
                        dve.bn_stats(st3[:, t, :], xs[:, t, :]).then_inc(e_ln, 1)
                    for t in range(NT):
                        dve.wait_ge(e_ln, t + 1)
                        dve.bn_aggr(mv3[:, t, :], st3[:, t, :]).then_inc(e_ln, 1)
                    dve.wait_ge(e_ln, 2 * NT)
                    inverse_deviation(dve, rs3[:, :], rw3[:, :], rt3[:, :], mv3[:, :, 1], e_ln, 2 * NT)
                    for t in range(NT):
                        dve.tensor_scalar(hs[:, t, :], xs[:, t, :], mv3[:, t, 0:1], rs3[:, t:t + 1],
                                          ALU.subtract, ALU.mult).then_inc(d_acc, E)
                    dve.wait_ge(e_T, 1)
                    dve.tensor_copy(cols[:, :], bank[0][:, 0:P]).then_inc(e_cols, 1)
                    dve.wait_ge(e_cols, 1)
                    dve.tensor_scalar(gain[:, :], cols[:, 0:LE], WS, None, ALU.mult).then_inc(e_gain, 1)
                    dve.wait_ge(e_fill, E + 4)
                    dve.wait_ge(e_rwh, 1)
                    dve.scalar_tensor_tensor(rwp[:, 1, :, :], rwf[:, :, :], WS, rwp[:, 0, :, :], ALU.mult, ALU.subtract)
                    flat = b2p[:, :, :].rearrange("p x h -> p (x h)")
                    dve.tensor_scalar(flat[0:1, :], b2f[0:1, :], WS, None, ALU.mult).then_inc(e_b2, 1)
                    dve.tensor_scalar(b2t[32:33, :], b2f[32:33, :], WS, None, ALU.mult).then_inc(e_b2, 1)
                    dve.wait_ge(e_b2, 2)
                    dve.scalar_tensor_tensor(flat[32:33, :], b2f[32:33, :], WS, b2t[32:33, :], ALU.mult, ALU.subtract)
                    dve.wait_ge(e_srw, 1)
                    dve.tensor_copy(srw[:, :, :].rearrange("p l e -> p (l e)"), bank[1][:, 0:LE])
                    dve.wait_ge(e_gain, 1)
                    for le in range(LE):
                        dve.wait_ge(e_h1, le + 1)
                        dve.scalar_tensor_tensor(w1p[:, 1, le, :], w1f[:, le, :], gain[:, le:le + 1], w1p[:, 0, le, :],
                                                 ALU.mult, ALU.subtract)
                    for l in range(L):
                        dve.wait_ge(e_h2, l + 1)
                        dve.scalar_tensor_tensor(w2p[:, 1, l * E:(l + 1) * E, :, :].rearrange("p e c h -> p (e c) h"),
                                                 w2f[:, l % 2, :, :], WS,
                                                 w2p[:, 0, l * E:(l + 1) * E, :, :].rearrange("p e c h -> p (e c) h"),
                                                 ALU.mult, ALU.subtract).then_inc(e_l2, 1)
                    dve.wait_ge(e_b1, 1)
                    dve.tensor_tensor(b1c[:, :, :].rearrange("p x c -> p (x c)"), bank[2][:, 0:LE * FC],
                                      cols[:, 64:64 + LE * FC], ALU.add)

                @block.tensor
                def _(pe):
                    pe.wait_ge(e_row, 48)
                    pe.transpose(bank[0][:, 0:P], rows[:, :], ident[:, :]).then_inc(e_T, 1)
                    pe.wait_ge(e_small, 64)
                    pe.wait_ge(e_fill, 2)
                    pe.matmul(bank[1][:, 0:LE], ones32[:, :], rwf[:, :, :].rearrange("p l e -> p (l e)"), start=True, stop=True
                              ).then_inc(e_srw, 1)
                    pe.wait_ge(e_cols, 1)
                    for le in range(LE):
                        if le % E == 0:
                            pe.wait_ge(e_w1[le // E], 16)
                        for c in range(FC):
                            last = pe.matmul(bank[2][:, le * FC + c:le * FC + c + 1], w1f[:, le, c * P:(c + 1) * P],
                                             cols[:, 32 + le:33 + le], start=True, stop=True)
                    last.then_inc(e_b1, 1)

        with ExitStack() as S:
            st4 = sb(S, "st4", [P, 4, 6], F32)
            mv4 = sb(S, "mv4", [P, 4, 2], F32)
            rs4, rw4, rt4, sd4 = (sb(S, f"rs4_{i}", [P, 4], F32) for i in range(4))
            xc = sb(S, "xc", [P, 4, D], F32)
            xh = [sb(S, f"xh{i}", [P, 4 * P], F16) for i in range(2)]
            xl = [sb(S, f"xl{i}", [P, 4 * P], F16) for i in range(2)]
            lg, lc, sL, z, th, sel, sel2, rank = (sb(S, n, [P, 4, E], F32)
                                                  for n in ("lg", "lc", "sL", "z", "th", "sel", "sel2", "rank"))
            top = sb(S, "top", [P, 4], F32)
            turn = sb(S, "turn", [P, 1], F32)
            gt, ge = (sb(S, n, [P, 4, E, E], F32) for n in ("gt", "ge"))
            comb = [sb(S, f"comb{i}", [P, 4, E], F32) for i in range(2)]
            gf = [sb(S, f"gf{i}", [P, FC, 4 * P], F32) for i in range(2)]
            gh = [sb(S, f"gh{i}", [P, FC, 4 * P], F16) for i in range(2)]
            gl = [sb(S, f"gl{i}", [P, FC, 4 * P], F16) for i in range(2)]
            hb = bank[0:4]
            yb = bank[4:6]
            tbk, lbk = bank[6], bank[7]
            d_ln, d_x, d_xT, d_xh, d_xl = sem("d_ln"), sem("d_x"), sem("d_xT"), sem("d_xh"), sem("d_xl")
            LNS = 8 + RSTD_STEPS
            d_lg, d_r, d_th, d_comb, d_comb2, d_sum = (sem("d_lg"), sem("d_r"), sem("d_th"), sem("d_comb"),
                                                       sem("d_comb2"), sem("d_sum"))
            d_h, d_g, d_hi, d_loP, d_loD, d_y = sem("d_h"), sem("d_g"), sem("d_hi"), sem("d_loP"), sem("d_loD"), sem("d_y")
            o_out = sem("o_out")
            RSTEPS = 14
            RAW = 2
            ACC0 = E * NT

            LAST = NBLK * (L - 1)

            class Step:
                def __init__(self, eng, it, c):
                    self.n, self.m2 = 2 * it + c, c % 2
                    self.layer, self.block = self.n // NBLK, self.n % NBLK
                    if not isinstance(self.n, int):
                        self.layer, self.block = eng.snap(self.layer), eng.snap(self.block)
                    self.unit = E * self.n

                def expert(self, e):
                    return bass.ds(E * self.layer + e, 1)

                def tile(self, k):
                    return bass.ds(4 * self.block + k, 1)

            class Unit:
                def __init__(self, step, e):
                    self.step, self.e, self.n, self.m2 = step, e, step.unit + e, e % 2

            def steps(eng, unit):

                def run(it, c, final, prepare=True, attend=True):
                    cur = Step(eng, it, c) if attend else None
                    nxt = Step(eng, it, c + 1) if prepare else None
                    before = None if isinstance(it, int) and c == 0 or not attend else Step(eng, it, c - 1) if isinstance(it, int) else \
                        Before(it, c - 1)
                    for e in range(E):
                        u = Unit(cur, e) if cur else None
                        v = Unit(cur, e - 1) if cur and e else Unit(before, E - 1) if before else None
                        unit(u, v, nxt, e, final)

                class Before:
                    def __init__(self, it, c):
                        self.n, self.m2, self.unit = 2 * it + c, c % 2, E * (2 * it + c)
                        self.layer, self.block = self.n // NBLK, self.n % NBLK
                        self.expert = lambda e: bass.ds(E * self.layer + e, 1)
                        self.tile = lambda k: bass.ds(4 * self.block + k, 1)

                run(0, -1, False, attend=False)
                run(0, 0, False)
                with eng.Fori(0, LAST // 2 - 1) as it:
                    for k in range(2):
                        run(it, 1 + k, False)
                with eng.Fori(LAST // 2 - 1, NSTEP // 2 - 1) as it:
                    for k in range(2):
                        run(it, 1 + k, True)
                run(0, NSTEP - 1, True, prepare=False)
                unit(None, Unit(Step(eng, 0, NSTEP - 1), E - 1), None, 0, True)

            with nc.Block() as block:
                @block.sync
                def _(sp):
                    for b in range(NBLK):
                        sp.wait_ge(d_acc, ACC0 + 4 * E * (LAST + b + 1))
                        sp.dma_start(out_tiles[:, 4 * b:4 * b + 4, :], hs[:, 4 * b:4 * b + 4, :]).then_inc(o_out, 16)
                    sp.wait_ge(o_out, 16 * NBLK)

                @block.gpsimd
                def _(pool):
                    def unit(u, v, f, e, final):
                        if u:
                            h = FC // 2
                            pool.wait_ge(d_hi, 2 * u.n + 1)
                            wait(pool, d_y, u.n - 1)
                            pool.tensor_tensor(gl[u.m2][:, 0:h, :], gf[u.m2][:, 0:h, :], gh[u.m2][:, 0:h, :],
                                               ALU.subtract).then_inc(d_loP, 1)
                    steps(pool, unit)

                @block.scalar
                def _(act):
                    def unit(u, v, f, e, final):
                        if u:
                            for c in range(FC):
                                act.wait_ge(d_h, FC * u.n + c + 1)
                                if c == 0:
                                    wait(act, d_loP, u.n - 1)
                                    wait(act, d_loD, u.n - 1)
                                act.activation(gf[u.m2][:, c, :], hb[c][:, :], ACT.Gelu, scale=1.0 / WS,
                                               bias=b1c[:, u.step.expert(u.e), c]).then_inc(d_g, 1)
                                if c % 2 == 1:
                                    wait(act, d_y, u.n - 1)
                                    act.wait_ge(d_g, FC * u.n + c + 1)
                                    act.activation(gh[u.m2][:, c - 1:c + 1, :], gf[u.m2][:, c - 1:c + 1, :],
                                                   ACT.Copy).then_inc(d_hi, 1)
                        if f and e == 1:
                            act.wait_ge(d_xT, f.n + 1)
                            wait(act, d_h, FC * E * (f.n - 1))
                            act.activation(xh[f.m2][:, :], tbk[:, :], ACT.Copy).then_inc(d_xh, 1)
                        if f and e == 3:
                            act.wait_ge(d_r, RSTEPS * (f.n + 1))
                            act.activation(th[:, :, :], z[:, :, :], ACT.Tanh).then_inc(d_th, 1)
                    steps(act, unit)

                @block.vector
                def _(dve):
                    def normalise(f, final):
                        base = LNS * f.n
                        dve.wait_ge(d_acc, 4 * E * f.n + 4 * E)
                        for k in range(4):
                            dve.bn_stats(st4[:, k, :], hs[:, f.tile(k), :].rearrange("p a c -> p (a c)")).then_inc(d_ln, 1)
                        dve.wait_ge(d_ln, base + 4)
                        dve.memset(turn[:, :], 0.0)
                        for k in range(4):
                            dve.bn_aggr(mv4[:, k, :], st4[:, k, :]).then_inc(d_ln, 1)
                        dve.wait_ge(d_ln, base + 8)
                        inverse_deviation(dve, rs4[:, :], rw4[:, :], rt4[:, :], mv4[:, :, 1], d_ln, base + 8)
                        wait(dve, d_xT, f.n)
                        for k in range(4):
                            dve.tensor_scalar(xc[:, k, :], hs[:, f.tile(k), :].rearrange("p a c -> p (a c)"),
                                              mv4[:, k, 0:1], rs4[:, k:k + 1], ALU.subtract, ALU.mult).then_inc(d_x, 1)
                        if final:
                            blk = bass.ds(4 * f.block, 4)
                            dve.wait_ge(d_x, 4 * f.n + 4)
                            dve.tensor_tensor(hs[:, blk, :], hs[:, blk, :], xs[:, blk, :], ALU.add).then_inc(d_sum, 1)

                    def low_half(u):
                        h = FC // 2
                        dve.wait_ge(d_hi, 2 * u.n + 2)
                        wait(dve, d_y, u.n - 1)
                        dve.tensor_tensor(gl[u.m2][:, h:FC, :], gf[u.m2][:, h:FC, :], gh[u.m2][:, h:FC, :],
                                          ALU.subtract).then_inc(d_loD, 1)

                    def combine(v, final):
                        dve.wait_ge(d_y, v.n + 1)
                        dve.wait_ge(d_acc, 4 * v.n + ACC0)
                        dve.wait_ge(d_comb, v.step.n + 1)
                        if final and v.e == 0:
                            due = v.step.n - LAST + 2
                            dve.wait_ge(d_sum, min(due, NBLK) if isinstance(due, int) else due)
                        for k in range(4):
                            t = hs[:, v.step.tile(k), :].rearrange("p a c -> p (a c)")
                            dve.scalar_tensor_tensor(t, yb[v.m2][:, k * D:(k + 1) * D], comb[v.step.m2][:, k, v.e:v.e + 1],
                                                     t, ALU.mult, ALU.add).then_inc(d_acc, 1)

                    def route(f):
                        base = RSTEPS * f.n
                        wide = lambda t: t.unsqueeze(2).broadcast_to((P, 4, E))
                        per_layer = lambda t: t[:, bass.ds(f.layer, 1), :].broadcast_to((P, 4, E))
                        other = lambda t: t[:, :, :].unsqueeze(2).broadcast_to((P, 4, E, E))
                        own = lambda t: t[:, :, :].unsqueeze(3).broadcast_to((P, 4, E, E))
                        dve.tensor_tensor(sd4[:, :], rw4[:, :], rs4[:, :], ALU.mult).then_inc(d_r, 1)
                        dve.tensor_tensor(lc[:, :, :], wide(mv4[:, :, 0]), per_layer(srw), ALU.mult).then_inc(d_r, 1)
                        dve.wait_ge(d_r, base + 2)
                        dve.tensor_tensor(lc[:, :, :], lc[:, :, :], per_layer(rbR), ALU.add).then_inc(d_r, 1)
                        dve.wait_ge(d_lg, f.n + 1)
                        dve.tensor_tensor(lg[:, :, :], lbk[:, 0:4 * E].rearrange("p (t e) -> p t e", t=4), wide(sd4[:, :]),
                                          ALU.mult).then_inc(d_r, 1)
                        dve.wait_ge(d_r, base + 4)
                        dve.scalar_tensor_tensor(lg[:, :, :], lg[:, :, :], 1.0 / WS, lc[:, :, :], ALU.mult, ALU.add).then_inc(d_r, 1)
                        dve.wait_ge(d_r, base + 5)
                        dve.tensor_tensor(gt[:, :, :, :], other(lg), own(lg), ALU.is_gt).then_inc(d_r, 1)
                        dve.tensor_tensor(ge[:, :, :, :], other(lg), own(lg), ALU.is_ge).then_inc(d_r, 1)
                        dve.wait_ge(d_r, base + 7)
                        dve.tensor_tensor(ge[:, :, :, :], ge[:, :, :, :], lower[:, :, :].unsqueeze(1).broadcast_to((P, 4, E, E)),
                                          ALU.mult).then_inc(d_r, 1)
                        dve.wait_ge(d_r, base + 8)
                        dve.tensor_tensor(gt[:, :, :, :], gt[:, :, :, :], ge[:, :, :, :], ALU.max).then_inc(d_r, 1)
                        dve.wait_ge(d_r, base + 9)
                        dve.tensor_reduce(rank[:, :, :], gt[:, :, :, :], AX.X, ALU.add).then_inc(d_r, 1)
                        dve.wait_ge(d_r, base + 10)
                        dve.tensor_scalar(sel[:, :, :], rank[:, :, :], 1.5, None, ALU.is_lt).then_inc(d_r, 1)
                        dve.wait_ge(d_r, base + 11)
                        dve.tensor_tensor(sL[:, :, :], sel[:, :, :], lg[:, :, :], ALU.mult).then_inc(d_r, 1)
                        dve.wait_ge(d_r, base + 12)
                        dve.tensor_reduce(top[:, :], sL[:, :, :], AX.X, ALU.add).then_inc(d_r, 1)
                        dve.wait_ge(d_r, base + 13)
                        dve.scalar_tensor_tensor(z[:, :, :], wide(top[:, :]), -0.5, lg[:, :, :], ALU.mult, ALU.add).then_inc(d_r, 1)

                    def unit(u, v, f, e, final):
                        if f and e == 0:
                            normalise(f, final)
                        if u:
                            low_half(u)
                        if f and e == 1:
                            dve.wait_ge(d_xh, f.n + 1)
                            dve.tensor_tensor(xl[f.m2][:, :], tbk[:, :], xh[f.m2][:, :], ALU.subtract).then_inc(d_xl, 1)
                        if f and e == 2:
                            route(f)
                        if v:
                            combine(v, final)
                        if f and e == 3:
                            dve.tensor_scalar(sel2[:, :, :], sel[:, :, :], 0.5 / WS, None, ALU.mult).then_inc(d_comb2, 1)
                            dve.wait_ge(d_comb2, f.n + 1)
                            dve.wait_ge(d_th, f.n + 1)
                            dve.scalar_tensor_tensor(comb[f.m2][:, :, :], th[:, :, :], 1.0, sel2[:, :, :],
                                                     ALU.add, ALU.mult).then_inc(d_comb, 1)
                    steps(dve, unit)

                @block.tensor
                def _(pe):
                    def hidden(u):
                        if u.e == 0:
                            pe.wait_ge(d_xl, u.step.n + 1)
                        x = (xh, xl, xh)
                        for c in range(FC):
                            wait(pe, d_g, FC * (u.n - 1) + c + 1)
                            for k, part in enumerate((0, 0, 1)):
                                last = pe.matmul(hb[c][:, :], w1p[:, part, u.step.expert(u.e), c * P:(c + 1) * P].rearrange("p a f -> p (a f)"),
                                                 x[k][u.step.m2][:, :], start=(k == 0), stop=(k == 2))
                            last.then_inc(d_h, 1)

                    def outputs(v):
                        wait(pe, d_acc, 4 * v.n + (ACC0 - 4))
                        le = v.step.expert(v.e)
                        pe.matmul(yb[v.m2][:, :], ones[:, :], b2p[:, le, :].broadcast_to((P, 4, D)), start=True, stop=False,
                                  skip_group_check=True)
                        for c in range(FC):
                            if c == 0:
                                pe.wait_ge(d_loP, v.n + 1)
                            if c == FC // 2:
                                pe.wait_ge(d_loD, v.n + 1)
                            for t in range(4):
                                for k, part in enumerate((0, 1, 0)):
                                    g = (gh, gh, gl)[k][v.m2]
                                    last = pe.matmul(yb[v.m2][:, t * D:(t + 1) * D], g[:, c, t * P:(t + 1) * P],
                                                     w2p[:, part, le, c, :].rearrange("p a h -> p (a h)"),
                                                     start=False, stop=(c == FC - 1 and k == 2), skip_group_check=True)
                        last.then_inc(d_y, 1)

                    def unit(u, v, f, e, final):
                        if u:
                            hidden(u)
                        if f and e == 1:
                            pe.wait_ge(d_x, 4 * f.n + 4)
                            wait(pe, d_xl, f.n)
                            for k in range(4):
                                last = pe.transpose(tbk[:, k * P:(k + 1) * P], xc[:, k, :], ident[:, :])
                            last.then_inc(d_xT, 1)
                        if f and e == 2:
                            pe.wait_ge(d_xl, f.n + 1)
                            wait(pe, d_r, RSTEPS * f.n)
                            for t in range(4):
                                for k, part in enumerate((0, 1, 0)):
                                    x = (xh, xh, xl)[k][f.m2]
                                    last = pe.matmul(lbk[:, t * E:(t + 1) * E], x[:, t * P:(t + 1) * P],
                                                     rwp[:, part, bass.ds(f.layer, 1), :].rearrange("p a e -> p (a e)"),
                                                     start=(k == 0), stop=(k == 2))
                            last.then_inc(d_lg, 1)
                        if v:
                            outputs(v)
                    steps(pe, unit)



_INS = ['x', 'ctx_1024', 'mask_Bx1x1xS2_if1', 'L0_xattn_Wq', 'L0_xattn_bq', 'L0_xattn_Wk', 'L0_xattn_bk',
        'L0_xattn_Wv', 'L0_xattn_bv', 'L0_xattn_Wo', 'L0_xattn_bo', 'L0_attn_W_qkv', 'L0_attn_b_qkv',
        'L0_attn_W_out', 'L0_attn_b_out', 'L0_ffn_router_w', 'L0_ffn_router_b', 'L0_ffn_ln_g', 'L0_ffn_ln_b',
        'L0_ffn_w1', 'L0_ffn_b1', 'L0_ffn_w2', 'L0_ffn_b2']


def kernel(**inputs):
    import numpy as np
    import concourse.bacc as bacc
    from concourse.bass_utils import run_bass_kernel_spmd

    nc = bacc.Bacc("TRN2", target_bir_lowering=False, num_devices=1)
    arrays, args = {}, []
    for name in _INS:
        a = np.ascontiguousarray(inputs[name])
        arrays[f"in_{name}_dram"] = a
        args.append(nc.dram_tensor(f"in_{name}_dram", a.shape, mybir.dt.from_np(a.dtype), kind="ExternalInput").ap())
    shape = inputs["x"].shape
    args.append(nc.dram_tensor("out_dram", shape, F32, kind="ExternalOutput").ap())
    build(nc, *args)
    r = run_bass_kernel_spmd(nc, [arrays], core_ids=[0])
    return r.results[0]["out_dram"]
```

```python
from contextlib import ExitStack

import concourse.bass as bass
from concourse import mybir

F32 = mybir.dt.float32
F16 = mybir.dt.float16
I32 = mybir.dt.int32
ALU = mybir.AluOpType
ACT = mybir.ActivationFunctionType
AX = mybir.AxisListType

P = 128
D = 128
H = 16
DH = D // H
G = 4
GH = H // G
GD = GH * DH
SQ = 32
EPS = 1e-5
MASKED = -60000.0
RSQRT_SEED = float(0x5F3759DF)


def wait(eng, sem, value):
    if not isinstance(value, int) or value > 0:
        eng.wait_ge(sem, value)


def emit_rstd(dve, rstd, work, var, done, base):
    dve.tensor_scalar(work, var, EPS, None, ALU.add).then_inc(done, 1)
    dve.wait_ge(done, base + 1)
    dve.tensor_scalar(rstd.bitcast(I32), work.bitcast(I32), 1, None, ALU.logical_shift_right).then_inc(done, 1)
    dve.wait_ge(done, base + 2)
    dve.tensor_scalar(rstd.bitcast(I32), rstd.bitcast(I32), -1.0, RSQRT_SEED, ALU.mult, ALU.add).then_inc(done, 1)
    return base + 3


def newton(dve, rstd, work, tmp, done, base):
    for k in range(3):
        dve.wait_ge(done, base + 3 * k)
        dve.tensor_tensor(tmp, rstd, rstd, ALU.mult).then_inc(done, 1)
        dve.wait_ge(done, base + 3 * k + 1)
        dve.scalar_tensor_tensor(tmp, tmp, -0.5, work, ALU.mult, ALU.mult).then_inc(done, 1)
        dve.wait_ge(done, base + 3 * k + 2)
        dve.scalar_tensor_tensor(rstd, tmp, 1.5, rstd, ALU.add, ALU.mult).then_inc(done, 1)
    return base + 9


RSTD_STEPS = 12


def inverse_deviation(dve, rstd, work, tmp, var, done, base):
    newton(dve, rstd, work, tmp, done, emit_rstd(dve, rstd, work, var, done, base))
    dve.wait_ge(done, base + RSTD_STEPS)


def build(nc, x, ctx, mask, Wq, bq, Wk, bk, Wv, bv, Wo, bo, W_qkv, b_qkv, W_out, b_out,
          router_w, router_b, ln_g, ln_b, w1, b1, w2, b2, out):
    B, _, _ = x.shape
    SK = ctx.shape[1]
    KM = SK - 1
    KC = KM // P
    T = B * SQ
    NT = T // P
    PB = P // SQ
    NPACK = B // PB
    NPAIR = PB // 2
    CW = GD + 1
    SCALE = float(DH) ** -0.5

    x_tiles = x.rearrange("b q c -> (b q) c").rearrange("(t p) c -> p t c", p=P)
    out_tiles = out.rearrange("b q c -> (b q) c").rearrange("(t p) c -> p t c", p=P)
    mask_d = mask.rearrange("b a c k -> (b a c) k")

    PARTS = 3
    q_d = nc.dram_tensor("q_parts_dram", [G, GD, PARTS, T], F16, kind="Internal").ap()
    k_d = nc.dram_tensor("k_parts_dram", [2, GD, PARTS, G, PB * KM], F16, kind="Internal").ap()
    kl_d = nc.dram_tensor("last_k_parts_dram", [GD, PARTS, G, B], F16, kind="Internal").ap()
    bias_d = nc.dram_tensor("mask_bias_dram", [B, KM], F16, kind="Internal").ap()
    biasl_d = nc.dram_tensor("last_mask_bias_dram", [B], F16, kind="Internal").ap()
    vlast_d = nc.dram_tensor("last_values_dram", [B, G * CW], F32, kind="Internal").ap()

    with ExitStack() as whole:
        def sb(scope, name, shape, dt):
            return scope.enter_context(nc.sbuf_tensor(name, shape, dt))

        def sem(name):
            return whole.enter_context(nc.semaphore(name))

        bank = [whole.enter_context(nc.psum_tensor(f"bank{i}", [P, 512], F32)) for i in range(8)]
        xs = sb(whole, "xs", [P, NT, D], F32)
        ident = sb(whole, "ident", [P, P], F32)
        WoM = sb(whole, "WoM", [P, GH, D], F32)
        rowsel = sb(whole, "rowsel", [P, GH], F32)
        boR = sb(whole, "boR", [P, D], F32)

        Wqkv = sb(whole, "Wqkv", [P, 3 * D], F32)
        Wout = sb(whole, "Wout", [P, D], F32)
        bqk_c = sb(whole, "bqk_c", [P, 2], F32)
        bv2_c = sb(whole, "bv2_c", [P, 1], F32)
        boutR = sb(whole, "boutR", [P, D], F32)
        st2 = sb(whole, "st2", [P, NT, 6], F32)
        c_w, c_st = sem("c_w"), sem("c_st")

        cross = whole.enter_context(ExitStack())
        WkT = sb(cross, "WkT", [P, D], F32)
        WvT = sb(cross, "WvT", [P, D], F32)
        bk_c = sb(cross, "bk_c", [P, 1], F32)
        maskT = sb(cross, "maskT", [P, KC, B], F16)
        KL = sb(cross, "KL", [P, G, B], F16)
        NROW = PARTS * GD
        KROW, SROW = NROW + 1, NROW + 2
        KS = [sb(cross, f"KS{i}", [P, G, PB, KM], F16) for i in range(4)]
        QS = [sb(cross, f"QS{i}", [P, G, GH, SQ, PB], F16) for i in range(4)]
        VX = [sb(cross, f"VX{i}", [P, PB, KC, 2, G, CW], F16) for i in range(4)]
        VL = [sb(cross, f"VL{i}", [P, PB, G, CW], F32) for i in range(4)]

        cx = [sb(cross, f"cx{i}", [P, PB, KC, D], F32) for i in range(2)]
        cxl = [sem(f"cxl{i}") for i in range(2)]

        def start_ctx(sp, p):
            sp.dma_start(cx[p.m2][:, :, :, :].rearrange("p b c d -> p b (c d)"),
                         ctx[bass.ds(PB * p.n, PB), 0:KM, :].rearrange("b (p c) d -> p b (c d)", c=KC)
                         ).then_inc(cxl[p.m2], 16)

        class Pack:
            def __init__(self, it, c):
                self.it, self.c = it, c
                self.n, self.m2, self.m4 = 4 * it + c, c % 2, c % 4
                self.d2, self.d4 = 2 * it + c // 2, it + c // 4

            def plus(self, k):
                return Pack(self.it, self.c + k)

            def after(self, k):
                return self.c >= k

        A = ExitStack()
        with A:
            w_nat = sb(A, "w_nat", [P, 4, D], F32)
            WqT = sb(A, "WqT", [P, D], F32)
            WoT = sb(A, "WoT", [P, D], F32)
            bq_c = sb(A, "bq_c", [P, 1], F32)
            bv_c = sb(A, "bv_c", [P, 1], F32)
            bvR = sb(A, "bvR", [P, D], F32)
            mask_i = sb(A, "mask_i", [P, SK], I32)
            m01 = sb(A, "m01", [P, SK], F32)
            bias16 = sb(A, "bias16", [P, SK], F16)
            clast = sb(A, "clast", [P, D], F32)
            clT = sb(A, "clT", [P, D], F32)
            klh = sb(A, "klh", [P, B], F16)
            kll = sb(A, "kll", [P, B], F16)
            vlast = sb(A, "vlast", [P, G, CW], F32)
            sel3 = sb(A, "sel3", [P, GH, G], F32)
            stats = sb(A, "stats", [P, NT, 6], F32)
            mv = sb(A, "mv", [P, NT, 2], F32)
            rstd = sb(A, "rstd", [P, NT], F32)
            nwt = sb(A, "nwt", [P, NT], F32)
            nw2 = sb(A, "nw2", [P, NT], F32)
            xn = [sb(A, f"xn{i}", [P, 4, D], F32) for i in range(2)]
            xnT = [sb(A, f"xnT{i}", [P, 4 * P], F32) for i in range(2)]
            q32 = [sb(A, f"q32_{i}", [P, 4 * P], F32) for i in range(2)]
            qh = [sb(A, f"qh{i}", [P, 4 * P], F16) for i in range(2)]
            ql = [sb(A, f"ql{i}", [P, 4 * P], F16) for i in range(2)]

            a_x = [sem("a_x0"), sem("a_x1")]
            a_w, a_out, a_kl = sem("a_w"), sem("a_out"), sem("a_kl")
            a_id, a_pool, a_fill = sem("a_id"), sem("a_pool"), sem("a_fill")
            a_wt, a_wtc, a_dve, a_pe = sem("a_wt"), sem("a_wtc"), sem("a_dve"), sem("a_pe")
            a_klh, a_last, a_kld = sem("a_klh"), sem("a_last"), sem("a_kld")
            a_st, a_ag, a_rs, a_xn = sem("a_st"), sem("a_ag"), sem("a_rs"), sem("a_xn")
            a_xT, a_xTc, a_q, a_q32, a_qh, a_ql = (sem("a_xT"), sem("a_xTc"), sem("a_q"),
                                                   sem("a_q32"), sem("a_qh"), sem("a_ql"))
            a_qd = [sem("a_qd0"), sem("a_qd1")]
            WD = 16 * 10

            def batch_first(t):
                return t[:, :].rearrange("p (k b q) -> p k q b", k=4, b=PB)

            def batch_last(t):
                return t[:, :].rearrange("p (k q b) -> p k q b", k=4, b=PB)

            def block_order(eng, front, back, ahead=1):
                half = NT // 8
                for u in range(ahead):
                    front(0, u)
                for u in range(2):
                    front(0, u + ahead)
                    back(0, u)
                with eng.Fori(1, half - 1) as it:
                    for u in range(2):
                        front(it, u + ahead)
                        back(it, u)
                for u in range(2):
                    if u + ahead < 2:
                        front(half - 1, u + ahead)
                    back(half - 1, u)

            with nc.Block() as block:
                @block.sync
                def _(sp):
                    for k, w in enumerate((Wq, Wk, Wv, Wo)):
                        sp.dma_start(w_nat[:, k, :], w).then_inc(a_w, 16)
                    for dst, src in ((bq_c, bq), (bk_c, bk), (bv_c, bv)):
                        sp.dma_start(dst[:, :], src.rearrange("(p a) -> p a", a=1)).then_inc(a_w, 16)
                    sp.dma_start(boR[:, :], bo.rearrange("(a n) -> a n", a=1).broadcast_to((P, D))).then_inc(a_w, 16)
                    sp.dma_start(mask_i[:, :], mask_d).then_inc(a_w, 16)
                    sp.dma_start(clast[:, :], ctx[:, KM, :]).then_inc(a_w, 16)
                    for i in range(2):
                        h = slice(i * NT // 2, (i + 1) * NT // 2)
                        sp.dma_start(xs[:, h, :], x_tiles[:, h, :]).then_inc(a_x[i], 16)
                    sp.dma_start(Wqkv[:, :], W_qkv).then_inc(c_w, 16)
                    sp.dma_start(Wout[:, :], W_out).then_inc(c_w, 16)
                    for k in range(2):
                        sp.dma_start(bqk_c[:, k:k + 1], b_qkv[k * D:(k + 1) * D].rearrange("(p a) -> p a", a=1)).then_inc(c_w, 16)
                    sp.dma_start(bv2_c[:, :], b_qkv[2 * D:3 * D].rearrange("(p a) -> p a", a=1)).then_inc(c_w, 16)
                    sp.dma_start(boutR[:, :], b_out.rearrange("(a n) -> a n", a=1).broadcast_to((P, D))).then_inc(c_w, 16)
                    sp.wait_ge(a_dve, 4)
                    sp.dma_start(bias_d, bias16[:, 0:KM]).then_inc(a_out, 16)
                    sp.dma_start(biasl_d.rearrange("(b a) -> b a", a=1), bias16[:, KM:SK]).then_inc(a_out, 16)
                    for g in range(G):
                        sp.wait_ge(a_out, 32)
                        sp.dma_start(KL[NROW:KROW, g, :],
                                     biasl_d.rearrange("(a b) -> a b", a=1)).then_inc(a_kl, 16)
                    sp.wait_ge(a_last, 2)
                    for part, src in ((0, klh), (1, kll), (2, klh)):
                        sp.dma_start(kl_d[:, part, :, :].rearrange("i g b -> g i b"), src[:, :]).then_inc(a_kld, 16)
                    sp.wait_ge(a_kld, 16 * PARTS)
                    sp.dma_start(KL[0:NROW, :, :].rearrange("r g b -> r (g b)"),
                                 kl_d.rearrange("i s g b -> (i s) (g b)")).then_inc(a_kl, 16)
                    for n in range(2):
                        start_ctx(sp, Pack(0, n))
                    sp.wait_ge(a_last, 4)
                    sp.dma_start(vlast_d, vlast[:, :, :].rearrange("p g c -> p (g c)")).then_inc(a_out, 16)
                    with sp.Fori(0, NT // 8) as it:
                        for u in range(2):
                            sp.wait_ge(a_ql, 2 * it + u + 1)
                            for part, src in ((0, qh), (1, qh), (2, ql)):
                                sp.dma_start(q_d[:, :, part, bass.ds((2 * it + u) * 4 * P, 4 * P)],
                                             src[u][:, :]).then_inc(a_qd[u], 16)
                    sp.wait_ge(a_out, 48)
                    sp.wait_ge(a_kl, 16 * (G + 1))
                    for u in range(2):
                        sp.wait_ge(a_qd[u], 16 * PARTS * (NT // 8))

                @block.gpsimd
                def _(pool):
                    pool.memset(ident[:, :], 0.0).then_inc(a_id, 1)
                    pool.memset(sel3[:, :, :], 1.0).then_inc(a_id, 1)
                    pool.wait_ge(a_id, 2)
                    pool.affine_select(out=ident[:, :], in_=ident[:, :], compare_op=ALU.not_equal, fill=1.0,
                                       base=0, pattern=[[-1, P]], channel_multiplier=1).then_inc(a_id, 1)
                    pool.affine_select(out=sel3[:, :, :], in_=sel3[:, :, :], compare_op=ALU.is_ge, fill=0.0,
                                       base=0, pattern=[[-DH, GH], [-GD, G]], channel_multiplier=1).then_inc(a_pool, 1)
                    pool.wait_ge(a_pool, 1)
                    pool.affine_select(out=sel3[:, :, :], in_=sel3[:, :, :], compare_op=ALU.is_ge, fill=0.0,
                                       base=DH - 1, pattern=[[DH, GH], [GD, G]], channel_multiplier=-1).then_inc(a_pool, 1)
                    pool.wait_ge(a_pool, 2)
                    n = 0
                    for i in range(4):
                        for part, value in ((QS[i][0:96, :, :, :, :].rearrange("p g h q b -> p (g h q b)").bitcast(F32), 0.0), (QS[i][96:98, :, :, :, :], 1.0),
                                            (KS[i][96:98, :, :, :], 1.0), (VX[i][:, :, :, 1, :, GD:CW], 0.0)):
                            pool.memset(part, value).then_inc(a_fill, 1)
                            n += 1
                            pool.wait_ge(a_fill, n)

                @block.scalar
                def _(act):
                    act.wait_ge(a_pe, 1)
                    act.wait_ge(a_w, WD)
                    act.activation(klh[:, :], bank[1][:, 0:B], ACT.Identity, bias=bk_c[:, 0:1]).then_inc(a_klh, 1)

                    def front(it, c):
                        n, m2 = 2 * it + c, c % 2
                        act.wait_ge(a_xT, n + 1)
                        wait(act, a_q, n - 1)
                        act.activation(xnT[m2][:, :], bank[2 + m2][:, :], ACT.Copy).then_inc(a_xTc, 1)

                    def back(it, u):
                        act.wait_ge(a_q32, 2 * it + u + 1)
                        wait(act, a_qd[u], 16 * PARTS * it)
                        act.activation(batch_last(qh[u]), batch_first(q32[u]), ACT.Copy).then_inc(a_qh, 1)
                    block_order(act, front, back)

                @block.vector
                def _(dve):
                    dve.wait_ge(a_w, WD)
                    dve.tensor_scalar(bias16[:, 0:KM].rearrange("b (c i) -> b i c", c=KC),
                                      mask_i[:, 0:KM].rearrange("b (i c) -> b i c", c=KC), 0.0, MASKED,
                                      ALU.is_equal, ALU.mult).then_inc(a_dve, 1)
                    dve.tensor_scalar(bias16[:, KM:SK], mask_i[:, KM:SK], 0.0, MASKED, ALU.is_equal, ALU.mult).then_inc(a_dve, 1)
                    dve.tensor_scalar(m01[:, :], mask_i[:, :], 0.0, None, ALU.not_equal).then_inc(a_dve, 1)
                    dve.tensor_copy(bvR[:, :], bv_c[:, 0:1].broadcast_to((P, D))).then_inc(a_dve, 1)
                    dve.wait_ge(a_wt, 1)
                    for k, w in enumerate((WqT, WkT, WvT, WoT)):
                        dve.tensor_copy(w[:, :], bank[0][:, k * D:(k + 1) * D]).then_inc(a_wtc, 1)
                    dve.wait_ge(a_wt, 2)
                    dve.tensor_copy(clT[:, :], bank[1][:, 0:P]).then_inc(a_wtc, 1)
                    dve.tensor_copy(maskT[:, :, :], bank[1][:, P:P + KC * B].rearrange("p (c b) -> p c b", c=KC)).then_inc(a_wtc, 1)
                    dve.wait_ge(a_pool, 2)
                    dve.tensor_reduce(rowsel[:, :], sel3[:, :, :], AX.X, ALU.max).then_inc(a_wtc, 1)
                    dve.wait_ge(a_wtc, 7)
                    for j in range(GH):
                        dve.tensor_scalar(WoM[:, j, :], WoT[:, :], rowsel[:, j:j + 1], None, ALU.mult).then_inc(a_wtc, 1)
                    dve.wait_ge(a_klh, 1)
                    dve.scalar_tensor_tensor(kll[:, :], bank[1][:, 0:B], bk_c[:, 0:1], klh[:, :],
                                             ALU.add, ALU.subtract).then_inc(a_last, 2)
                    dve.wait_ge(a_pe, 3)
                    dve.tensor_copy(vlast[:, :, 0:GD], bank[5][:, 0:D].rearrange("p (g c) -> p g c", g=G)).then_inc(a_last, 1)
                    dve.tensor_copy(vlast[:, :, GD:CW], m01[:, KM:SK].unsqueeze(1).broadcast_to((P, G, 1))).then_inc(a_last, 1)
                    for t in range(NT):
                        if t % (NT // 2) == 0:
                            dve.wait_ge(a_x[t // (NT // 2)], 16)
                        dve.bn_stats(stats[:, t, :], xs[:, t, :]).then_inc(a_st, 1)
                    for t in range(NT):
                        dve.wait_ge(a_st, t + 1)
                        dve.bn_aggr(mv[:, t, :], stats[:, t, :]).then_inc(a_ag, 1)
                    dve.wait_ge(a_ag, NT)
                    inverse_deviation(dve, rstd[:, :], nwt[:, :], nw2[:, :], mv[:, :, 1], a_rs, 0)

                    def front(it, c):
                        n, m2 = 2 * it + c, c % 2
                        wait(dve, a_xT, n - 1)
                        for k in range(4):
                            t = 4 * n + k
                            dve.tensor_scalar(xn[m2][:, k, :], xs[:, bass.ds(t, 1), :], mv[:, bass.ds(t, 1), 0],
                                              rstd[:, bass.ds(t, 1)], ALU.subtract, ALU.mult).then_inc(a_xn, 1)

                    def back(it, u):
                        dve.wait_ge(a_q, 2 * it + u + 1)
                        dve.tensor_scalar(q32[u][:, :], bank[4 + u][:, :], bq_c[:, 0:1], SCALE,
                                          ALU.add, ALU.mult).then_inc(a_q32, 1)
                        dve.wait_ge(a_qh, 2 * it + u + 1)
                        wait(dve, a_qd[u], 16 * PARTS * it)
                        dve.tensor_tensor(batch_last(ql[u]), batch_first(q32[u]), batch_last(qh[u]), ALU.subtract).then_inc(a_ql, 1)
                    block_order(dve, front, back, 2)
                    dve.wait_ge(a_pe, 2)
                    dve.tensor_tensor(boR[:, :], boR[:, :], bank[6][:, 0:D], ALU.add)

                @block.tensor
                def _(pe):
                    pe.wait_ge(a_w, WD)
                    pe.wait_ge(a_id, 3)
                    for k in range(4):
                        last = pe.transpose(bank[0][:, k * D:(k + 1) * D], w_nat[:, k, :], ident[:, :])
                    last.then_inc(a_wt, 1)
                    pe.wait_ge(a_dve, 4)
                    pe.transpose(bank[1][:, 0:P], clast[:, :], ident[:, :])
                    for c in range(KC):
                        last = pe.transpose(bank[1][:, P + c * B:P + (c + 1) * B], m01[:, c:KM:KC], ident[:, :])
                    last.then_inc(a_wt, 1)
                    pe.wait_ge(a_wtc, 6)
                    pe.matmul(bank[1][:, 0:B], WkT[:, :], clT[:, :], start=True, stop=True).then_inc(a_pe, 1)
                    pe.matmul(bank[6][:, 0:D], bvR[:, :], WoT[:, :], start=True, stop=True).then_inc(a_pe, 1)
                    pe.matmul(bank[5][:, 0:D], clT[:, :], WvT[:, :], start=True, stop=True).then_inc(a_pe, 1)
                    pe.wait_ge(a_last, 3)

                    def front(it, c):
                        n, m2 = 2 * it + c, c % 2
                        for k in range(4):
                            pe.wait_ge(a_xn, 4 * n + k + 1)
                            last = pe.transpose(bank[2 + m2][:, k * P:(k + 1) * P], xn[m2][:, k, :], ident[:, :])
                        last.then_inc(a_xT, 1)

                    def back(it, u):
                        pe.wait_ge(a_xTc, 2 * it + u + 1)
                        wait(pe, a_q32, 2 * it + u - 1)
                        pe.matmul(bank[4 + u][:, :], WqT[:, :], xnT[u][:, :], start=True, stop=True).then_inc(a_q, 1)
                    block_order(pe, front, back)

        with ExitStack() as S:
            cT = [sb(S, f"cT{i}", [P, 2 * KM], F32) for i in range(2)]
            kh = [sb(S, f"kh{i}", [P, PB, KM], F16) for i in range(2)]
            kl = [sb(S, f"kl{i}", [P, PB, KM], F16) for i in range(2)]
            p32 = [sb(S, f"p32_{i}", [P, KC, 512], F32) for i in range(2)]
            ph = [sb(S, f"ph{i}", [P, KC, 512], F16) for i in range(4)]
            pl = [sb(S, f"pl{i}", [P, KC, 512], F16) for i in range(4)]
            mx = [sb(S, f"mx{i}", [P, G, PB], F32) for i in range(2)]
            KLP = [sb(S, f"KLP{i}", [P, G, PB], F16) for i in range(2)]
            nm16 = [sb(S, f"nm16_{i}", [P, G, PB], F16) for i in range(2)]
            sl = [sb(S, f"sl{i}", [P, G, PB], F32) for i in range(2)]
            plast = [sb(S, f"plast{i}", [P, G, PB], F32) for i in range(2)]
            tl = [sb(S, f"tl{i}", [P, PB, G, CW], F32) for i in range(2)]
            osum = [sb(S, f"osum{i}", [P, 2, G, CW], F32) for i in range(2)]
            orec = [sb(S, f"orec{i}", [P, 2, G], F32) for i in range(2)]
            on = [sb(S, f"on{i}", [P, 2, G, GD], F32) for i in range(2)]
            oT = sb(S, "oT", [P, GH, PB, SQ], F32)

            ksl = [sem(f"ksl{i}") for i in range(4)]
            ksw = [sem(f"ksw{i}") for i in range(2)]
            qsl = [sem(f"qsl{i}") for i in range(4)]
            mrl = [sem(f"mrl{i}") for i in range(4)]
            vll = [sem(f"vll{i}") for i in range(4)]
            KSN, QSN, MRN = 16 * 2, 16 * GH, 16 * G
            tb_ready, tb_read = sem("tb_ready"), sem("tb_read")
            kb_ready, kh_done, kl_done = sem("kb_ready"), sem("kh_done"), sem("kl_done")
            vb_ready, vh_done, vl_done = sem("vb_ready"), sem("vh_done"), sem("vl_done")
            vm_done, kp_done, b_bias = sem("vm_done"), sem("kp_done"), sem("b_bias")
            r_ready, r_read = [sem("r_ready0"), sem("r_ready1")], [sem("r_read0"), sem("r_read1")]
            sl_ready, m_step, plast_done = sem("sl_ready"), sem("m_step"), sem("plast_done")
            t_ready, t_read = [sem("t_ready0"), sem("t_ready1")], [sem("t_read0"), sem("t_read1")]
            ph_done, pl_done, pv_done = sem("ph_done"), sem("pl_done"), sem("pv_done")
            tl_done, o_step = sem("tl_done"), sem("o_step")
            ot_ready, ot_read, y_ready, y_read = sem("ot_ready"), sem("ot_read"), sem("y_ready"), sem("y_read")

            RB, TBK, WB, OB, MB = bank[0:2], bank[2:4], bank[4:6], bank[6], bank[7]
            LB = OB[:, 2 * G * CW:2 * G * CW + G * PB]
            last_scores = LB.rearrange("p (g b) -> p g b", g=G)
            YB = MB[:, 0:D]
            MSTEPS, OSTEPS = 3, 3
            ND = 3
            NR = 2

            def steps(eng, step):
                def peeled(s):
                    pk = lambda n: Pack(0, n) if 0 <= n < NPACK else None
                    step(pk(s), pk(s + NR), pk(s + ND), pk(s - 1), pk(s + 1), pk(s + ND + 1))
                for s in range(-ND - 1, 2):
                    peeled(s)
                full = (NPACK - ND - 4) // 4
                with eng.Fori(0, full) as it:
                    for k in range(4):
                        step(*(Pack(it, 2 + k + d) for d in (0, NR, ND, -1, 1, ND + 1)))
                for s in range(2 + 4 * full, NPACK + 1):
                    peeled(s)

            with nc.Block() as block:
                @block.sync
                def _(sp):
                    def load_ctx(p):
                        if p.after(2):
                            sp.wait_ge(tb_ready, 2 * p.n - 2)
                        start_ctx(sp, p)

                    def step(a, r, p, prev, nxt, q):
                        if p:
                            if p.after(4):
                                sp.wait_ge(t_ready[1], PB * (p.n - 3))
                                sp.wait_ge(tl_done, p.n - 3)
                            for j in range(GH):
                                rows = DH * PARTS
                                sp.dma_start(QS[p.m4][rows * j:rows * (j + 1), :, j, :, :].rearrange("i g q b -> i g (q b)"),
                                             q_d[:, DH * j:DH * (j + 1), :, bass.ds(P * p.n, P)]
                                             .rearrange("g d s q -> (d s) g q")).then_inc(qsl[p.m4], 16)
                            sp.dma_start(KS[p.m4][NROW:KROW, :, :, :].rearrange("o g b k -> o g (b k)"),
                                         bias_d[bass.ds(PB * p.n, PB), :].rearrange("b (o k) -> o (b k)", o=1)
                                         .unsqueeze(1).broadcast_to((1, G, PB * KM))).then_inc(ksl[p.m4], 16)
                            sp.dma_start(VL[p.m4][:, :, :, :].rearrange("p b g c -> p (b g c)"),
                                         vlast_d[bass.ds(PB * p.n, PB), :].rearrange("b (a n) -> a (b n)", a=1)
                                         .broadcast_to((P, PB * G * CW))).then_inc(vll[p.m4], 16)
                        if nxt:
                            sp.wait_ge(m_step, MSTEPS * nxt.n + 2)
                            for g in range(G):
                                sp.dma_start(QS[nxt.m4][SROW - 1:SROW, g, :, :, :].rearrange("o h q b -> o (h q b)"),
                                             nm16[nxt.m2][:, g, :]).then_inc(mrl[nxt.m4], 16)
                        if p:
                            sp.wait_ge(kl_done, 2 * p.n + 2)
                            sp.wait_ge(kh_done, 2 * p.n + 2)
                            for part, src in ((0, kh), (1, kl), (2, kh)):
                                sp.dma_start(k_d[p.m2, :, part, :, :].rearrange("i g n -> g i n"),
                                             src[p.m2][:, :, :].rearrange("p b k -> p (b k)")).then_inc(ksw[p.m2], 16)
                            sp.wait_ge(ksw[p.m2], 16 * PARTS * (p.d2 + 1))
                            sp.dma_start(KS[p.m4][0:NROW, :, :, :].rearrange("r g b k -> r (g b k)"),
                                         k_d[p.m2].rearrange("i s g n -> (i s) (g n)")).then_inc(ksl[p.m4], 16)
                            if not isinstance(p.n, int) or p.n + 2 < NPACK:
                                load_ctx(p.plus(2))

                    steps(sp, step)

                @block.gpsimd
                def _(pool):
                    def step(a, r, p, prev, nxt, q):
                        if r:
                            wait(pool, sl_ready, r.n - 1)
                            pool.tensor_copy(KLP[r.m2][0:KROW, :, :], KL[0:KROW, :, bass.ds(PB * r.n, PB)]).then_inc(kp_done, 1)
                        for j in range(PB if a else 0):
                            n = PB * a.n + j
                            pool.wait_ge(ph_done, n + 1)
                            if a.after(1):
                                pool.wait_ge(pv_done, n - 3)
                            pool.tensor_tensor(pl[j][:, :, :], p32[j % 2][:, :, :], ph[j][:, :, :],
                                               ALU.subtract).then_inc(pl_done, 1)
                            if j == 1:
                                pool.wait_ge(vll[a.m4], 16 * (a.d4 + 1))
                                pool.wait_ge(plast_done, a.n + 1)
                                if a.after(2):
                                    pool.wait_ge(o_step, OSTEPS * 2 * (a.n - 1))
                                for b in range(PB):
                                    last = pool.tensor_tensor(tl[a.m2][:, b, :, :], VL[a.m4][:, b, :, :],
                                                              plast[a.m2][:, :, b:b + 1].broadcast_to((P, G, CW)), ALU.mult)
                                last.then_inc(tl_done, 1)
                        if p:
                            if p.after(4):
                                pool.wait_ge(pv_done, PB * (p.n - 3))
                            pool.tensor_copy(VX[p.m4][:, :, :, 0, :, GD],
                                             maskT[:, :, bass.ds(PB * p.n, PB)].rearrange("p c b -> p b c")
                                             .unsqueeze(3).broadcast_to((P, PB, KC, G))).then_inc(vm_done, 1)
                    pool.tensor_tensor(xs[:, :, :], xs[:, :, :], boR[:, :].unsqueeze(1).broadcast_to((P, NT, D)),
                                       ALU.add).then_inc(b_bias, 1)
                    steps(pool, step)

                @block.scalar
                def _(act):
                    def exps(a, j):
                        n = PB * a.n + j
                        if a.after(1) or j >= 2:
                            act.wait_ge(pl_done, n - 1)
                        if a.after(1):
                            act.wait_ge(pv_done, n - 3)
                        act.wait_ge(t_ready[0], n + 1)
                        act.activation(p32[j % 2][:, 0, :], TBK[0][:, :], ACT.Exp)
                        act.activation(ph[j][:, 0, :], TBK[0][:, :], ACT.Exp).then_inc(t_read[0], 1)
                        act.wait_ge(t_ready[1], n + 1)
                        act.activation(p32[j % 2][:, 1, :], TBK[1][:, :], ACT.Exp).then_inc(t_read[1], 1)

                    def keys(p, u):
                        act.wait_ge(kb_ready, 2 * p.n + u + 1)
                        if u == 0 and (p.after(2)):
                            act.wait_ge(ksw[p.m2], 16 * PARTS * p.d2)
                        act.activation(kh[p.m2][:, 2 * u:2 * u + 2, :], WB[1 - u][:, :].rearrange("p (b k) -> p b k", b=2),
                                       ACT.Identity, bias=bk_c[:, 0:1]).then_inc(kh_done, 1)

                    def values(p, u):
                        act.wait_ge(vb_ready, 2 * p.n + u + 1)
                        if u == 0 and (p.after(4)):
                            act.wait_ge(pv_done, PB * (p.n - 3))
                        act.activation(VX[p.m4][:, 2 * u:2 * u + 2, :, 0, :, 0:GD].rearrange("p b c g d -> p (b c) g d"),
                                       WB[u][:, :].rearrange("p (x g d) -> p x g d", x=2 * KC, g=G),
                                       ACT.Copy).then_inc(vh_done, 1)

                    def context(p, u):
                        q = 2 * p.n + u
                        act.wait_ge(tb_ready, q + 1)
                        if p.after(1):
                            act.wait_ge(vb_ready, q - 1)
                        act.activation(cT[u][:, :], WB[u][:, :], ACT.Copy).then_inc(tb_read, 1)

                    def gather_o(pk, u):
                        act.wait_ge(ot_ready, 2 * pk.n + u + 1)
                        if u == 0 and (pk.after(1)):
                            act.wait_ge(y_ready, pk.n)
                        act.activation(oT[:, :, 2 * u:2 * u + 2, :].rearrange("p h b q -> p b h q"),
                                       MB[:, 0:256].rearrange("p (b h q) -> p b h q", b=2, h=GH),
                                       ACT.Copy).then_inc(ot_read, 1)

                    def step(a, r, p, prev, nxt, q):
                        for j in range(PB):
                            if a:
                                exps(a, j)
                            if j % 2 == 0 and p:
                                keys(p, j // 2)
                            if j % 2 == 0 and prev:
                                gather_o(prev, j // 2)
                            if j == 1 and p:
                                context(p, 1)
                            if j % 2 == 1 and p:
                                values(p, j // 2)
                            if j == 3 and q:
                                context(q, 0)
                            if j == 2 and nxt:
                                act.wait_ge(m_step, MSTEPS * (nxt.n + 1))
                                if nxt.after(2):
                                    act.wait_ge(tl_done, nxt.n - 1)
                                act.activation(plast[nxt.m2][:, :, :], sl[nxt.m2][:, :, :], ACT.Exp).then_inc(plast_done, 1)
                    steps(act, step)

                @block.vector
                def _(dve):
                    def maxima(r, j):
                        for hf in range(2):
                            dve.wait_ge(r_ready[hf], PB * r.n + j + 1)
                            dve.tensor_reduce(mx[r.m2][:, 2 * hf:2 * hf + 2, j], RB[hf][:, :].rearrange("p (g k) -> p g k", g=2),
                                              AX.X, ALU.max).then_inc(r_read[hf], 1)

                    def join_last_key(r):
                        dve.wait_ge(sl_ready, r.n + 1)
                        if r.after(2):
                            dve.wait_ge(pv_done, PB * r.plus(-1).n)
                        dve.wait_ge(r_read[1], PB * r.n + PB)
                        dve.tensor_tensor(mx[r.m2][:, :, :], last_scores, mx[r.m2][:, :, :], ALU.max).then_inc(m_step, 1)

                    def negate_maxima(r):
                        dve.wait_ge(m_step, MSTEPS * r.n + 1)
                        if r.after(2):
                            dve.wait_ge(mrl[r.plus(-2).m4], MRN * (r.plus(-2).d4 + 1))
                        dve.tensor_scalar(nm16[r.m2][:, :, :], mx[r.m2][:, :, :], -1.0, None, ALU.mult).then_inc(m_step, 1)

                    def shift_last_key(r):
                        dve.wait_ge(m_step, MSTEPS * r.n + 2)
                        if r.after(2):
                            dve.wait_ge(plast_done, r.n - 1)
                        dve.tensor_tensor(sl[r.m2][:, :, :], last_scores, nm16[r.m2][:, :, :], ALU.add).then_inc(m_step, 1)

                    def low_keys(p, u):
                        dve.wait_ge(kh_done, 2 * p.n + u + 1)
                        dve.scalar_tensor_tensor(kl[p.m2][:, 2 * u:2 * u + 2, :].rearrange("p b k -> p (b k)"),
                                                 WB[1 - u][:, :], bk_c[:, 0:1],
                                                 kh[p.m2][:, 2 * u:2 * u + 2, :].rearrange("p b k -> p (b k)"),
                                                 ALU.add, ALU.subtract).then_inc(kl_done, 1)

                    def low_values(p, u):
                        dve.wait_ge(vh_done, 2 * p.n + u + 1)
                        v = VX[p.m4][:, 2 * u:2 * u + 2, :, :, :, 0:GD].rearrange("p b c s g d -> p (b c) s g d")
                        dve.tensor_tensor(v[:, :, 1], WB[u][:, :].rearrange("p (x g d) -> p x g d", x=2 * KC, g=G),
                                          v[:, :, 0], ALU.subtract).then_inc(vl_done, 1)

                    def high_part(a, j):
                        dve.wait_ge(t_read[1], PB * a.n + j + 1)
                        dve.tensor_copy(ph[j][:, 1, :], p32[j % 2][:, 1, :]).then_inc(ph_done, 1)

                    def sums(pk, u):
                        dve.wait_ge(pv_done, PB * pk.n + 2 * u + 2)
                        dve.wait_ge(tl_done, pk.n + 1)
                        dve.tensor_tensor(osum[u][:, :, :, :], OB[:, 0:2 * G * CW].rearrange("p (b g c) -> p b g c", b=2, g=G),
                                          tl[pk.m2][:, 2 * u:2 * u + 2, :, :], ALU.add).then_inc(o_step, 1)

                    def reciprocals(pk, u):
                        dve.wait_ge(o_step, OSTEPS * (2 * pk.n + u) + 1)
                        dve.reciprocal(orec[u][:, :, :], osum[u][:, :, :, GD]).then_inc(o_step, 1)

                    def quotients(pk, u):
                        dve.wait_ge(o_step, OSTEPS * (2 * pk.n + u) + 2)
                        if pk.after(1):
                            dve.wait_ge(ot_ready, 2 * pk.n + u - 1)
                        dve.tensor_tensor(on[u][:, :, :, :], osum[u][:, :, :, 0:GD],
                                          orec[u][:, :, :].unsqueeze(3).broadcast_to((P, 2, G, GD)),
                                          ALU.mult).then_inc(o_step, 1)

                    def step(a, r, p, prev, nxt, q):
                        for j in range(PB):
                            if j < 2 and nxt:
                                maxima(nxt, j + 2)
                            if j >= 2 and r:
                                maxima(r, j - 2)
                            pk, u = {1: (prev, 1), 3: (a, 0)}.get(j, (None, 0))
                            if j == 1 and nxt:
                                join_last_key(nxt)
                            if pk:
                                sums(pk, u)
                            if j == 1 and nxt:
                                negate_maxima(nxt)
                            if pk:
                                reciprocals(pk, u)
                            if j == 1 and nxt:
                                shift_last_key(nxt)
                            if a and j != 1:
                                high_part(a, j)
                            if j == 1 and p:
                                low_values(p, 0)
                            if a and j == 1:
                                high_part(a, j)
                            if pk:
                                quotients(pk, u)
                            if j % 2 == 0 and p:
                                low_keys(p, j // 2)
                            if j == 3 and p:
                                low_values(p, 1)
                            if j == 3 and prev:
                                dve.wait_ge(b_bias, 1)
                                dve.wait_ge(y_ready, prev.n + 1)
                                dve.tensor_tensor(xs[:, bass.ds(prev.n, 1), :], YB.unsqueeze(1),
                                                  xs[:, bass.ds(prev.n, 1), :], ALU.add).then_inc(y_read, 1)
                                dve.wait_ge(y_read, prev.n + 1)
                                dve.bn_stats(st2[:, bass.ds(prev.n, 1), :].rearrange("p a s -> p (a s)"),
                                             xs[:, bass.ds(prev.n, 1), :].rearrange("p a c -> p (a c)")).then_inc(c_st, 1)
                    steps(dve, step)

                @block.tensor
                def _(pe):
                    def transposed_context(p, u):
                        q = 2 * p.n + u
                        if u == 0:
                            pe.wait_ge(cxl[p.m2], 16 * (p.d2 + 1))
                        wait(pe, kl_done, q)
                        for k in range(2 * KC):
                            last = pe.transpose(WB[u][:, k * P:(k + 1) * P], cx[p.m2][:, 2 * u + k // KC, k % KC, :], ident[:, :])
                        last.then_inc(tb_ready, 1)

                    def project(p, u):
                        q = 2 * p.n + u
                        pe.wait_ge(tb_read, q + 1)
                        wait(pe, vl_done, q)
                        pe.matmul(WB[1 - u][:, :], WkT[:, :], cT[u][:, :], start=True, stop=True).then_inc(kb_ready, 1)
                        for k in range(2 * KC):
                            last = pe.matmul(WB[u][:, k * D:(k + 1) * D], cT[u][:, k * P:(k + 1) * P], WvT[:, :],
                                             start=True, stop=True)
                        last.then_inc(vb_ready, 1)

                    def queries(pk, g, b, rows):
                        return QS[pk.m4][0:rows, g, :, :, b].rearrange("k h q -> k (h q)")

                    def row_scores(r, j):
                        if j == 0:
                            pe.wait_ge(ksl[r.m4], KSN * (r.d4 + 1))
                            pe.wait_ge(qsl[r.m4], QSN * (r.d4 + 1))
                        for hf in range(2):
                            wait(pe, r_read[hf], PB * r.n + j)
                            for g in (2 * hf, 2 * hf + 1):
                                last = pe.matmul(RB[hf][:, (g % 2) * KM:(g % 2 + 1) * KM], queries(r, g, j, KROW),
                                                 KS[r.m4][0:KROW, g, j, :], start=True, stop=True)
                            last.then_inc(r_ready[hf], 1)

                    def last_key_scores(r):
                        pe.wait_ge(kp_done, r.n + 1)
                        wait(pe, m_step, MSTEPS * r.n)
                        if r.after(2):
                            pe.wait_ge(o_step, OSTEPS * 2 * r.plus(-2).n + 1)
                        for g in range(G):
                            for b in range(PB):
                                last = pe.matmul(LB[:, g * PB + b:g * PB + b + 1], queries(r, g, b, KROW),
                                                 KLP[r.m2][0:KROW, g, b:b + 1], start=True, stop=True)
                        last.then_inc(sl_ready, 1)

                    def scores(a, j):
                        if j == 0:
                            pe.wait_ge(mrl[a.m4], MRN * (a.d4 + 1))
                        for c in range(KC):
                            wait(pe, t_read[c], PB * a.n + j)
                            for g in range(G):
                                last = pe.matmul(TBK[c][:, g * P:(g + 1) * P], KS[a.m4][0:SROW, g, j, c * P:(c + 1) * P],
                                                 queries(a, g, j, SROW), start=True, stop=True)
                            last.then_inc(t_ready[c], 1)

                    def outputs(pk, j):
                        n = PB * pk.n + j
                        pe.wait_ge(pl_done, n + 1)
                        if j == 0:
                            pe.wait_ge(vl_done, 2 * pk.n + 2)
                            pe.wait_ge(vm_done, pk.n + 1)
                        if j % 2 == 0:
                            m = 2 * pk.n + j // 2
                            if pk.after(1) or j:
                                pe.wait_ge(o_step, OSTEPS * m - 2)
                        for g in range(G):
                            o = OB[:, (j % 2 * G + g) * CW:(j % 2 * G + g + 1) * CW]
                            for c in range(KC):
                                v = VX[pk.m4][:, j, c, :, g, :]
                                hi, lo = (s[j][:, c, g * P:(g + 1) * P] for s in (ph, pl))
                                pe.matmul(o, hi, v[:, 0, :], start=(c == 0), stop=False)
                                pe.matmul(o, hi, v[:, 1, :], start=False, stop=False)
                                last = pe.matmul(o, lo, v[:, 0, :], start=False, stop=(c == KC - 1))
                        last.then_inc(pv_done, 1)

                    def transposed_outputs(pk, u):
                        pe.wait_ge(o_step, OSTEPS * (2 * pk.n + u + 1))
                        wait(pe, *((y_read, pk.n), (ot_read, 2 * pk.n + 1))[u])
                        for b in range(2):
                            last = pe.transpose(MB[:, b * P:(b + 1) * P], on[u][:, b, :, :].rearrange("p g d -> p (g d)"), ident[:, :])
                        last.then_inc(ot_ready, 1)

                    def step(a, r, p, prev, nxt, q):
                        for j in range(PB):
                            if a:
                                scores(a, j)
                            if j < 2 and nxt:
                                row_scores(nxt, j + 2)
                            if j >= 2 and r:
                                row_scores(r, j - 2)
                            if j == 0 and nxt:
                                last_key_scores(nxt)
                            if j == 1 and p:
                                transposed_context(p, 1)
                            if j == 3 and q:
                                transposed_context(q, 0)
                            if j < 2 and prev:
                                outputs(prev, j + 2)
                            if j >= 2 and a:
                                if j == 2 and nxt:
                                    pe.wait_ge(m_step, MSTEPS * (nxt.n + 1))
                                outputs(a, j - 2)
                            if j % 2 == 0 and p:
                                project(p, j // 2)
                            if j % 2 == 0 and prev:
                                transposed_outputs(prev, j // 2)
                            if j == 3 and prev:
                                pe.wait_ge(ot_read, 2 * prev.n + 2)
                                for h in range(GH):
                                    last = pe.matmul(YB[:, :], oT[:, h, :, :].rearrange("p b q -> p (b q)"), WoM[:, h, :],
                                                     start=(h == 0), stop=(h == GH - 1))
                                last.then_inc(y_ready, 1)
                    steps(pe, step)

        cross.close()

        L, E, _, F = w1.shape
        FC = F // P
        LE = L * E
        SHIFT = 2
        w1p = sb(whole, "w1p", [P, LE + SHIFT, 2, F], F16)
        w2p = sb(whole, "w2p", [P, LE + SHIFT, 2, FC, D], F16)
        w1f = w1p[:, :, :, :].rearrange("p x s f -> p (x s f)").bitcast(F32).rearrange("p (x f) -> p x f", f=F)
        w2f = w2p[:, :, :, :, :].rearrange("p x s c h -> p (x s c h)").bitcast(F32).rearrange("p (x f) -> p x f", f=F)
        rwf = sb(whole, "rwf", [P, L, E], F32)
        rows = sb(whole, "rows", [P, P], F32)
        b2f = sb(whole, "b2f", [P, D], F32)
        rbR = sb(whole, "rbR", [P, L, E], F32)
        e_row, e_small, e_w = sem("e_row"), sem("e_small"), sem("e_w")
        with ExitStack() as S:
            E3 = 3 * D
            NB4 = 4 * PB
            NBLK = NT // 4
            WoutM = sb(S, "WoutM", [P, GH, D], F32)
            bv2R = sb(S, "bv2R", [P, D], F32)
            mv2 = sb(S, "mv2", [P, NT, 2], F32)
            rs2, rw2, rt2 = (sb(S, f"rs2_{i}", [P, NT], F32) for i in range(3))
            xm = sb(S, "xm", [P, 4, D], F32)
            xmT = sb(S, "xmT", [P, 4 * P], F32)
            qkh = [[sb(S, f"qkh{i}{k}", [P, 4 * P], F16) for k in range(2)] for i in range(2)]
            qkl = [[sb(S, f"qkl{i}{k}", [P, 4 * P], F16) for k in range(2)] for i in range(2)]
            vn = [sb(S, f"vn{i}", [P, 4, D], F32) for i in range(2)]
            Q2 = [sb(S, f"Q2_{i}", [NROW, G, GH, SQ, NB4], F16) for i in range(2)]
            K2 = [sb(S, f"K2_{i}", [NROW, G, 4 * P], F16) for i in range(2)]
            V2 = [sb(S, f"V2_{i}", [P, NB4, G, GD], F32) for i in range(2)]
            dif = [sb(S, f"dif{i}", [P, PB, G, SQ], F32) for i in range(2)]
            mx2 = [sb(S, f"mx2_{i}", [P, PB, G], F32) for i in range(2)]
            sm2 = [sb(S, f"sm2_{i}", [P, PB, G], F32) for i in range(4)]
            rc2 = [sb(S, f"rc2_{i}", [P, PB, G], F32) for i in range(4)]
            pr = [sb(S, f"pr{i}", [P, PB, G, SQ], F32) for i in range(4)]
            pT = [sb(S, f"pT{i}", [P, PB * P], F32) for i in range(2)]
            oT2 = [sb(S, f"oT2_{i}", [P, GH, PB, SQ], F32) for i in range(2)]

            q2_d = nc.dram_tensor("q2_parts_dram", [2, G, GD, PARTS, 4 * P], F16, kind="Internal").ap()
            k2_d = nc.dram_tensor("k2_parts_dram", [2, G, GD, PARTS, 4 * P], F16, kind="Internal").ap()
            v2_d = nc.dram_tensor("v2_dram", [2, NB4, SQ, D], F32, kind="Internal").ap()

            c_wm, c_pool, c_b, c_bias = sem("c_wm"), sem("c_pool"), sem("c_b"), sem("c_bias")
            c_ln, c_xm = sem("c_ln"), sem("c_xm")
            c_xT, c_xTc, c_pq, c_pv = sem("c_xT"), sem("c_xTc"), sem("c_pq"), sem("c_pv")
            c_hi, c_lo, c_vn = sem("c_hi"), sem("c_lo"), sem("c_vn")
            c_wr = [sem(f"c_wr{i}") for i in range(2)]
            c_vw = [sem(f"c_vw{i}") for i in range(2)]
            c_qk = [sem(f"c_qk{i}") for i in range(2)]
            c_v2 = [sem(f"c_v2{i}") for i in range(2)]
            c_s, c_mx, c_dif, c_exp, c_sum, c_rc, c_nrm = (sem("c_s"), sem("c_mx"), sem("c_dif"), sem("c_exp"),
                                                           sem("c_sum"), sem("c_rc"), sem("c_nrm"))
            c_tr, c_trc, c_o, c_oc, c_y, c_yr = (sem("c_tr"), sem("c_trc"), sem("c_o"), sem("c_oc"),
                                                 sem("c_y"), sem("c_yr"))
            WRN = 16 * 2 * PARTS

            class Step:
                def __init__(self, it, c):
                    self.it, self.c, self.s = it, c, 2 * it + c

                def block(self, k):
                    b = Tokens4(self.it, self.c + k)
                    return b if not isinstance(b.n, int) or 0 <= b.n < NBLK else None

                def tile(self, k):
                    n = 4 * self.s + k
                    return n if not isinstance(n, int) or 0 <= n < NT else None

            class Tokens4:
                def __init__(self, it, c):
                    self.n, self.m2, self.d2 = 2 * it + c, c % 2, it + c // 2

            def blocks(step):
                def run(eng):
                    for s in range(-2, 1):
                        step(Step(0, s))
                    full = (NBLK - 3) // 2
                    with eng.Fori(0, full) as it:
                        for k in range(2):
                            step(Step(it, 1 + k))
                    for s in range(1 + 2 * full, NBLK + 1):
                        step(Step(0, s))
                return run

            def side_by_side(st, w):
                return tuple(st.tile(w + k) for k in (2, 1, 0, -1, -2))

            with nc.Block() as block:
                @block.sync
                def _(sp):
                    sp.wait_ge(c_pool, 5)
                    sp.dma_start(rows[0:LE, :], ln_g.rearrange("l e h -> (l e) h")).then_inc(e_row, 16)
                    sp.dma_start(rows[32:32 + LE, :], ln_b.rearrange("l e h -> (l e) h")).then_inc(e_row, 16)
                    sp.dma_start(rows[64:64 + LE * FC, :], b1.rearrange("l e (c f) -> (l e c) f", f=P)).then_inc(e_row, 16)
                    sp.dma_start(rwf[:, :, :], router_w.rearrange("l h e -> h l e")).then_inc(e_small, 16)
                    sp.dma_start(rbR[:, :, :].rearrange("p l e -> p (l e)"),
                                 router_b.rearrange("(a l) e -> a (l e)", a=1).broadcast_to((P, LE))).then_inc(e_small, 16)
                    for r in (0, 32):
                        sp.dma_start(b2f[r:r + LE, :], b2.rearrange("l e h -> (l e) h")).then_inc(e_small, 16)
                    w1_rows = w1.rearrange("l e h f -> h (l e) f")
                    w2_rows = w2.rearrange("l e (c f) h -> f (l e c) h", f=P)

                    def step(st):
                        f = st.block(2)
                        v = st.block(1)
                        if v:
                            wait(sp, c_o, 4 * (v.n - 1))
                            sp.wait_ge(c_vw[v.m2], 16 * (v.d2 + 1))
                            for g in range(G):
                                sp.dma_start(V2[v.m2][SQ * g:SQ * (g + 1), :, g, :],
                                             v2_d[v.m2, :, :, GD * g:GD * (g + 1)].rearrange("b k c -> k b c")
                                             ).then_inc(c_v2[v.m2], 16)
                        if f:
                            for k, dram in enumerate((q2_d, k2_d)):
                                sp.wait_ge(c_lo, 2 * f.n + k + 1)
                                for part in range(PARTS):
                                    src = (qkh, qkh, qkl)[part] if k == 0 else (qkh, qkl, qkh)[part]
                                    sp.dma_start(dram[f.m2, :, :, part, :].rearrange("g i n -> (g i) n"), src[f.m2][k][:, :]).then_inc(c_wr[f.m2], 16)
                            sp.wait_ge(c_vn, f.n + 1)
                            sp.dma_start(v2_d[f.m2].rearrange("(t b) k c -> (b k) t c", t=4), vn[f.m2][:, :, :]).then_inc(c_vw[f.m2], 16)
                            sp.wait_ge(c_wr[f.m2], WRN * (f.d2 + 1))
                            wait(sp, c_s, 4 * f.n - 4)
                            for j in range(GH):
                                rows = DH * PARTS
                                sp.dma_start(Q2[f.m2][rows * j:rows * (j + 1), :, j, :, :].rearrange("i g q b -> i g (q b)"),
                                             q2_d[f.m2, :, DH * j:DH * (j + 1), :, :].rearrange("g d s q -> (d s) g q")
                                             ).then_inc(c_qk[f.m2], 16)
                            sp.dma_start(K2[f.m2][:, :, :], k2_d[f.m2].rearrange("g i s n -> (i s) g n")).then_inc(c_qk[f.m2], 16)
                            n = LE // NBLK
                            own = bass.ds(n * f.n + SHIFT, n)
                            sp.dma_start(w1f[:, own, :], w1_rows[:, bass.ds(n * f.n, n), :]).then_inc(e_w, 16)
                            sp.dma_start(w2f[:, own, :].rearrange("p x (c h) -> p (x c) h", c=FC),
                                         w2_rows[:, bass.ds(FC * n * f.n, FC * n), :]).then_inc(e_w, 16)
                    blocks(step)(sp)
                    sp.wait_ge(e_row, 48)
                    sp.wait_ge(e_small, 64)
                    sp.wait_ge(e_w, 16 * 2 * NBLK)

                @block.gpsimd
                def _(pool):
                    pool.memset(rows[:, :], 0.0).then_inc(c_pool, 1)
                    for i in range(2):
                        pool.memset(Q2[i][:, :, :, :, :].rearrange("p g h q b -> p (g h q b)").bitcast(F32), 0.0).then_inc(c_pool, 1)
                        pool.memset(V2[i][:, :, :, :], 0.0).then_inc(c_pool, 1)

                    def step(st):
                        f = st.block(2)
                        for w in range(4):
                            sc, nm, tr, pv, y = side_by_side(st, w)
                            if f and w == 0:
                                pool.wait_ge(c_wm, 6)
                                pool.wait_ge(c_xm, 4 * f.n + 4)
                                blk = bass.ds(4 * f.n, 4)
                                pool.tensor_tensor(xs[:, blk, :], xs[:, blk, :], boutR[:, :].unsqueeze(1).broadcast_to((P, 4, D)),
                                                   ALU.add).then_inc(c_bias, 1)
                            if nm is not None:
                                i = (w + 1) % 4
                                pool.wait_ge(c_rc, nm + 1)
                                pool.tensor_tensor(pr[i][:, :, :, :], pr[i][:, :, :, :],
                                                   rc2[i][:, :, :].unsqueeze(3).broadcast_to((P, PB, G, SQ)),
                                                   ALU.mult).then_inc(c_nrm, 1)
                    pool.wait_ge(c_pool, 5)
                    blocks(step)(pool)

                def blocks_first(t):
                    return t.rearrange("p (b q) -> p q b", q=SQ)

                def blocks_last(t):
                    return t.rearrange("p (q b) -> p q b", q=SQ)

                @block.scalar
                def _(act):
                    def step(st):
                        f = st.block(2)
                        for w in range(4):
                            sc, nm, tr, pv, y = side_by_side(st, w)
                            if f and w == 0:
                                act.wait_ge(c_xT, f.n + 1)
                                act.activation(xmT[:, :], bank[0][:, :], ACT.Copy).then_inc(c_xTc, 1)
                            if f and w in (1, 2):
                                k = w - 1
                                act.wait_ge(c_pq, 2 * f.n + w)
                                wait(act, c_wr[f.m2], WRN * f.d2)
                                out = qkh[f.m2][k][:, :]
                                src = bank[1][:, :]
                                if k == 0:
                                    out, src = blocks_last(out), blocks_first(src)
                                act.activation(out, src, ACT.Identity, bias=bqk_c[:, k:k + 1]).then_inc(c_hi, 1)
                            if f and w == 3:
                                act.wait_ge(c_pv, f.n + 1)
                                wait(act, c_vw[f.m2], 16 * f.d2)
                                act.activation(vn[f.m2][:, :, :], bank[0][:, :].rearrange("p (t c) -> p t c", t=4),
                                               ACT.Copy).then_inc(c_vn, 1)
                            if tr is not None:
                                act.wait_ge(c_tr, tr + 1)
                                wait(act, c_o, tr - 1)
                                act.activation(pT[w % 2][:, :], bank[4 + w % 2][:, :], ACT.Copy).then_inc(c_trc, 1)
                            if pv is not None:
                                i = (w + 1) % 2
                                act.wait_ge(c_o, pv + 1)
                                wait(act, c_y, pv - 1)
                                act.activation(oT2[i][:, :, :, :].rearrange("p h b q -> p b h q"),
                                               bank[6][:, :].rearrange("p (b h q) -> p b h q", b=PB, h=GH),
                                               ACT.Copy).then_inc(c_oc, 1)
                            if sc is not None:
                                i = (w + 2) % 4
                                act.wait_ge(c_dif, sc + 1)
                                wait(act, c_tr, sc - 3)
                                act.activation(pr[i][:, :, :, :], dif[w % 2][:, :, :, :], ACT.Exp).then_inc(c_exp, 1)
                    blocks(step)(act)

                @block.vector
                def _(dve):
                    def normalise(f):
                        wait(dve, c_xT, f.n)
                        for k in range(4):
                            t = bass.ds(4 * f.n + k, 1)
                            dve.tensor_scalar(xm[:, k, :], xs[:, t, :].rearrange("p a c -> p (a c)"),
                                              mv2[:, t, 0], rs2[:, t], ALU.subtract, ALU.mult).then_inc(c_xm, 1)

                    dve.wait_ge(c_st, NT)
                    for t in range(NT):
                        dve.bn_aggr(mv2[:, t, :], st2[:, t, :]).then_inc(c_ln, 1)
                    dve.wait_ge(c_ln, NT)
                    inverse_deviation(dve, rs2[:, :], rw2[:, :], rt2[:, :], mv2[:, :, 1], c_ln, NT)
                    normalise(Tokens4(0, 0))
                    dve.wait_ge(c_w, 16 * 6)
                    dve.tensor_scalar(bv2R[:, :], bv2_c[:, 0:1].broadcast_to((P, D)), float(D) ** -0.5, None, ALU.mult).then_inc(c_wm, 1)
                    for j in range(GH):
                        dve.tensor_scalar(WoutM[:, j, :], Wout[:, :], rowsel[:, j:j + 1], float(D) ** -0.5,
                                          ALU.mult, ALU.mult).then_inc(c_wm, 1)
                    dve.wait_ge(c_b, 1)
                    dve.tensor_tensor(boutR[:, :], bank[7][:, 0:D], boutR[:, :], ALU.add).then_inc(c_wm, 1)

                    def step(st):
                        f = st.block(2)
                        for w in range(4):
                            sc, nm, tr, pv, y = side_by_side(st, w)
                            if sc is not None:
                                i = w % 2
                                sv = bank[2 + i][:, :].rearrange("p (b g k) -> p b g k", b=PB, g=G)
                                dve.wait_ge(c_s, sc + 1)
                                dve.tensor_reduce(mx2[i][:, :, :], sv, AX.X, ALU.max).then_inc(c_mx, 1)
                                dve.wait_ge(c_mx, sc + 1)
                                wait(dve, c_exp, sc - 1)
                                dve.tensor_tensor(dif[i][:, :, :, :], sv, mx2[i][:, :, :].unsqueeze(3).broadcast_to((P, PB, G, SQ)),
                                                  ALU.subtract).then_inc(c_dif, 1)
                            if w == 3 and st.block(3):
                                normalise(st.block(3))
                            if f and w in (1, 2):
                                k = w - 1
                                hi, lo, src = qkh[f.m2][k][:, :], qkl[f.m2][k][:, :], bank[1][:, :]
                                if k == 0:
                                    hi, lo, src = blocks_last(hi), blocks_last(lo), blocks_first(src)
                                dve.wait_ge(c_hi, 2 * f.n + w)
                                dve.scalar_tensor_tensor(lo, src, bqk_c[:, k:k + 1], hi, ALU.add, ALU.subtract).then_inc(c_lo, 1)
                            if nm is not None:
                                i = (w + 1) % 4
                                dve.wait_ge(c_exp, nm + 1)
                                dve.tensor_reduce(sm2[i][:, :, :], pr[i][:, :, :, :], AX.X, ALU.add).then_inc(c_sum, 1)
                                dve.wait_ge(c_sum, nm + 1)
                                dve.reciprocal(rc2[i][:, :, :], sm2[i][:, :, :]).then_inc(c_rc, 1)
                            if y is not None:
                                dve.wait_ge(c_y, y + 1)
                                dve.wait_ge(c_bias, (st.block(0) if w >= 2 else st.block(-1)).n + 1)
                                dve.tensor_tensor(xs[:, bass.ds(y, 1), :], bank[7][:, 0:D].unsqueeze(1),
                                                  xs[:, bass.ds(y, 1), :], ALU.add).then_inc(c_yr, 1)
                                dve.wait_ge(c_yr, y + 1)
                                dve.bn_stats(st2[:, bass.ds(y, 1), :].rearrange("p a s -> p (a s)"),
                                             xs[:, bass.ds(y, 1), :].rearrange("p a c -> p (a c)")).then_inc(c_st, 1)
                    blocks(step)(dve)

                @block.tensor
                def _(pe):
                    pe.wait_ge(c_w, 16 * 6)
                    pe.wait_ge(c_wm, 1)
                    pe.matmul(bank[7][:, 0:D], bv2R[:, :], Wout[:, :], start=True, stop=True).then_inc(c_b, 1)
                    pe.wait_ge(c_wm, 6)

                    def step(st):
                        f = st.block(2)
                        for w in range(4):
                            sc, nm, tr, pv, y = side_by_side(st, w)
                            if sc is not None:
                                bl = st.block((w + 2) // 4)
                                m = bl.m2
                                if w == 2:
                                    pe.wait_ge(c_qk[m], 16 * (GH + 1) * (bl.d2 + 1))
                                wait(pe, c_dif, sc - 1)
                                t = (w + 2) % 4
                                for b in range(PB):
                                    for g in range(G):
                                        last = pe.matmul(bank[2 + w % 2][:, (b * G + g) * SQ:(b * G + g + 1) * SQ],
                                                         Q2[m][:, g, :, :, t * PB + b].rearrange("k h q -> k (h q)"),
                                                         K2[m][:, g, (t * PB + b) * SQ:(t * PB + b + 1) * SQ], start=True, stop=True)
                                last.then_inc(c_s, 1)
                            if f and w == 0:
                                wait(pe, c_vn, f.n)
                                pe.wait_ge(c_xm, 4 * f.n + 4)
                                for k in range(4):
                                    last = pe.transpose(bank[0][:, k * P:(k + 1) * P], xm[:, k, :], ident[:, :])
                                last.then_inc(c_xT, 1)
                            if f and w in (1, 2):
                                pe.wait_ge(c_xTc, f.n + 1)
                                wait(pe, c_lo, 2 * f.n + w - 1)
                                pe.matmul(bank[1][:, :], Wqkv[:, (w - 1) * D:w * D], xmT[:, :], start=True, stop=True).then_inc(c_pq, 1)
                            if f and w == 3:
                                for k in range(4):
                                    last = pe.matmul(bank[0][:, k * D:(k + 1) * D], xmT[:, k * P:(k + 1) * P], Wqkv[:, 2 * D:E3],
                                                     start=True, stop=True)
                                last.then_inc(c_pv, 1)
                            if tr is not None:
                                pe.wait_ge(c_nrm, tr + 1)
                                wait(pe, c_trc, tr - 1)
                                for b in range(PB):
                                    last = pe.transpose(bank[4 + w % 2][:, b * P:(b + 1) * P],
                                                        pr[w][:, b, :, :].rearrange("p g k -> p (g k)"), ident[:, :])
                                last.then_inc(c_tr, 1)
                            if pv is not None:
                                bl = st.block((w - 1) // 4)
                                m = bl.m2
                                if w == 1:
                                    pe.wait_ge(c_v2[m], 16 * G * (bl.d2 + 1))
                                pe.wait_ge(c_trc, pv + 1)
                                wait(pe, c_oc, pv)
                                t = (w - 1) % 4
                                for b in range(PB):
                                    last = pe.matmul(bank[6][:, b * P:(b + 1) * P],
                                                     V2[m][:, t * PB + b, :, :].rearrange("k g c -> k (g c)"),
                                                     pT[(w + 1) % 2][:, b * P:(b + 1) * P], start=True, stop=True)
                                last.then_inc(c_o, 1)
                            if y is not None:
                                pe.wait_ge(c_oc, y + 1)
                                wait(pe, c_yr, y)
                                for h in range(GH):
                                    last = pe.matmul(bank[7][:, 0:D], oT2[w % 2][:, h, :, :].rearrange("p b q -> p (b q)"),
                                                     WoutM[:, h, :], start=(h == 0), stop=(h == GH - 1))
                                last.then_inc(c_y, 1)
                    blocks(step)(pe)

        NSTEP = L * NBLK
        WS = 64.0
        moe = whole.enter_context(ExitStack())
        hs = sb(moe, "hs", [P, NT, D], F32)
        rwp = sb(moe, "rwp", [P, 2, L, E], F16)
        b2p = sb(moe, "b2p", [P, D], F16)
        pick = sb(moe, "pick", [P, LE, P], F16)
        b1c = sb(moe, "b1c", [P, LE, FC], F32)
        srw = sb(moe, "srw", [P, L, E], F32)
        lower = sb(moe, "lower", [P, E, E], F32)
        gain = sb(moe, "gain", [P, LE], F32)
        e_h1, e_h2, e_lo1, e_lo2 = sem("e_h1"), sem("e_h2"), sem("e_lo1"), sem("e_lo2")

        def high_weights(act, le):
            x, own = bass.ds(le, 1), bass.ds(le + SHIFT, 1)
            wait(act, e_lo1, le - SHIFT + 1)
            act.activation(w1p[:, x, 0, :].rearrange("p a f -> p (a f)"), w1f[:, own, :].rearrange("p a f -> p (a f)"),
                           ACT.Copy, scale=gain[:, x]).then_inc(e_h1, 1)
            wait(act, e_lo2, le - SHIFT + 1)
            act.activation(w2p[:, x, 0, :, :].rearrange("p a c h -> p (a c h)"), w2f[:, own, :].rearrange("p a f -> p (a f)"),
                           ACT.Copy, scale=WS).then_inc(e_h2, 1)

        def low_weights(dve, le):
            x, own = bass.ds(le, 1), bass.ds(le + SHIFT, 1)
            dve.wait_ge(e_h1, le + 1)
            dve.scalar_tensor_tensor(w1p[:, x, 1, :].rearrange("p a f -> p (a f)"), w1f[:, own, :].rearrange("p a f -> p (a f)"),
                                     gain[:, x], w1p[:, x, 0, :].rearrange("p a f -> p (a f)"),
                                     ALU.mult, ALU.subtract).then_inc(e_lo1, 1)
            dve.wait_ge(e_h2, le + 1)
            dve.scalar_tensor_tensor(w2p[:, x, 1, :, :].rearrange("p a c h -> p (a c h)"), w2f[:, own, :].rearrange("p a f -> p (a f)"),
                                     WS, w2p[:, x, 0, :, :].rearrange("p a c h -> p (a c h)"),
                                     ALU.mult, ALU.subtract).then_inc(e_lo2, 1)

        with ExitStack() as S:
            b2t = sb(S, "b2t", [P, D], F16)
            ones32 = sb(S, "ones32", [P, P], F32)
            cols = sb(S, "cols", [P, P], F32)
            lnbd = sb(S, "lnbd", [P, LE, P], F32)
            b1r = sb(S, "b1r", [P, F], F32)
            nb3 = sb(S, "nb3", [P, NT], F32)
            mv3 = sb(S, "mv3", [P, NT, 2], F32)
            rs3, rw3, rt3 = (sb(S, f"rs3_{i}", [P, NT], F32) for i in range(3))
            e_fill, e_pick = sem("e_fill"), sem("e_pick")
            e_T, e_cols, e_gain, e_b1, e_srw = sem("e_T"), sem("e_cols"), sem("e_gain"), sem("e_b1"), sem("e_srw")
            e_rwh, e_b2, e_ln = sem("e_rwh"), sem("e_b2"), sem("e_ln")
            d_acc = sem("d_acc")

            with nc.Block() as block:
                @block.gpsimd
                def _(pool):
                    pool.memset(ones32[:, :], 1.0).then_inc(e_fill, 1)
                    pool.memset(lnbd[:, :, :], 0.0).then_inc(e_fill, 1)
                    pool.memset(pick[:, :, :], 0.0).then_inc(e_fill, 1)
                    pool.memset(b2p[:, :], 0.0).then_inc(e_fill, 1)
                    pool.memset(lower[:, :, :], 0.0).then_inc(e_fill, 1)
                    pool.wait_ge(e_fill, 5)
                    for e in range(1, E):
                        pool.memset(lower[:, e, 0:e], 1.0).then_inc(e_fill, 1)
                    for r in (0, 32):
                        pool.affine_select(out=pick[:, :, :], in_=pick[:, :, :], compare_op=ALU.not_equal, fill=1.0,
                                           base=-r, pattern=[[-1, LE], [0, P]], channel_multiplier=1).then_inc(e_pick, 1)
                        pool.wait_ge(e_pick, 1 + r // 32)

                @block.scalar
                def _(act):
                    act.activation(rwp[:, 0, :, :], rwf[:, :, :], ACT.Copy, scale=WS).then_inc(e_rwh, 1)
                    act.wait_ge(e_gain, 1)
                    for e in range(E):
                        high_weights(act, e)
                    act.wait_ge(e_ln, NT + RSTD_STEPS + 1)
                    for t in range(NT // 2):
                        act.activation(hs[:, t, :], xs[:, t, :], ACT.Identity, scale=rs3[:, t:t + 1],
                                       bias=nb3[:, t:t + 1]).then_inc(d_acc, E)

                @block.vector
                def _(dve):
                    dve.wait_ge(e_T, 1)
                    dve.tensor_copy(cols[:, :], bank[0][:, 0:P]).then_inc(e_cols, 1)
                    dve.wait_ge(e_cols, 1)
                    dve.tensor_scalar(gain[:, :], cols[:, 0:LE], WS, None, ALU.mult).then_inc(e_gain, 1)
                    dve.wait_ge(e_fill, 2)
                    dve.tensor_copy(lnbd[:, :, :].rearrange("p x m -> p (x m)")[:, 0:LE * P:P + 1], cols[:, 32:32 + LE]).then_inc(e_cols, 1)
                    dve.wait_ge(c_st, 2 * NT)
                    for t in range(NT):
                        dve.bn_aggr(mv3[:, t, :], st2[:, t, :]).then_inc(e_ln, 1)
                    dve.wait_ge(e_ln, NT)
                    inverse_deviation(dve, rs3[:, :], rw3[:, :], rt3[:, :], mv3[:, :, 1], e_ln, NT)
                    dve.scalar_tensor_tensor(nb3[:, :], mv3[:, :, 0], -1.0, rs3[:, :], ALU.mult, ALU.mult).then_inc(e_ln, 1)
                    dve.wait_ge(e_fill, E + 4)
                    dve.wait_ge(e_rwh, 1)
                    low = slice(32, 32 + LE)
                    dve.tensor_scalar(b2p[0:LE, :], b2f[0:LE, :], WS, None, ALU.mult)
                    dve.tensor_scalar(b2t[low, :], b2f[low, :], WS, None, ALU.mult).then_inc(e_b2, 1)
                    dve.wait_ge(e_b2, 1)
                    dve.scalar_tensor_tensor(b2p[low, :], b2f[low, :], WS, b2t[low, :], ALU.mult, ALU.subtract)
                    dve.scalar_tensor_tensor(rwp[:, 1, :, :], rwf[:, :, :], WS, rwp[:, 0, :, :], ALU.mult, ALU.subtract)
                    dve.wait_ge(e_srw, 1)
                    dve.tensor_copy(srw[:, :, :].rearrange("p l e -> p (l e)"), bank[1][:, 0:LE])
                    for e in range(E):
                        dve.wait_ge(e_b1, e + 1)
                        low_weights(dve, e)
                    for t in range(NT // 2, NT):
                        dve.tensor_scalar(hs[:, t, :], xs[:, t, :], mv3[:, t, 0:1], rs3[:, t:t + 1],
                                          ALU.subtract, ALU.mult).then_inc(d_acc, E)
                    dve.wait_ge(e_b1, LE)
                    dve.tensor_copy(b1r[:, :], bank[2][:, 0:F]).then_inc(e_cols, 1)
                    dve.wait_ge(e_T, 2)
                    dve.tensor_tensor(b1c[:, :, :].rearrange("p x c -> p c x"),
                                      bank[3][:, :].rearrange("p (c x) -> p c x", c=FC)[:, :, 0:LE],
                                      cols[:, 64:64 + LE * FC].rearrange("p (x c) -> p c x", c=FC), ALU.add)

                @block.tensor
                def _(pe):
                    pe.transpose(bank[0][:, 0:P], rows[:, :], ident[:, :]).then_inc(e_T, 1)
                    pe.wait_ge(e_fill, 1)
                    pe.matmul(bank[1][:, 0:LE], ones32[:, :], rwf[:, :, :].rearrange("p l e -> p (l e)"), start=True, stop=True
                              ).then_inc(e_srw, 1)
                    pe.wait_ge(e_cols, 2)
                    for le in range(LE):
                        pe.matmul(bank[2][:, 0:F], lnbd[:, le, :], w1f[:, le + SHIFT, :], start=(le == 0),
                                  stop=(le == LE - 1)).then_inc(e_b1, 1)
                    pe.wait_ge(e_cols, 3)
                    for c in range(FC):
                        last = pe.transpose(bank[3][:, c * P:(c + 1) * P], b1r[:, c * P:(c + 1) * P], ident[:, :])
                    last.then_inc(e_T, 1)

        with ExitStack() as S:
            st4 = sb(S, "st4", [P, 4, 6], F32)
            mv4 = sb(S, "mv4", [P, 4, 2], F32)
            rs4, rw4, rt4, sd4 = (sb(S, f"rs4_{i}", [P, 4], F32) for i in range(4))
            xc = sb(S, "xc", [P, 4, D], F32)
            xh = [sb(S, f"xh{i}", [P, 4 * P], F16) for i in range(2)]
            xl = [sb(S, f"xl{i}", [P, 4 * P], F16) for i in range(2)]
            lg, lc, sL, z, th, sel, sel2, rank = (sb(S, n, [P, 4, E], F32)
                                                  for n in ("lg", "lc", "sL", "z", "th", "sel", "sel2", "rank"))
            top = sb(S, "top", [P, 4], F32)
            turn = sb(S, "turn", [P, 1], F32)
            gt, ge = (sb(S, n, [P, 4, E, E], F32) for n in ("gt", "ge"))
            comb = [sb(S, f"comb{i}", [P, 4, E], F32) for i in range(2)]
            gf = [sb(S, f"gf{i}", [P, FC, 4 * P], F32) for i in range(2)]
            gh = [sb(S, f"gh{i}", [P, FC, 4 * P], F16) for i in range(2)]
            gl = [sb(S, f"gl{i}", [P, FC, 4 * P], F16) for i in range(2)]
            hb = bank[0:4]
            yb = bank[4:6]
            tbk, lbk = bank[6], bank[7]
            d_ln, d_x, d_xT, d_xh, d_xl = sem("d_ln"), sem("d_x"), sem("d_xT"), sem("d_xh"), sem("d_xl")
            LNS = 8 + RSTD_STEPS
            d_lg, d_r, d_th, d_comb, d_comb2, d_sum = (sem("d_lg"), sem("d_r"), sem("d_th"), sem("d_comb"),
                                                       sem("d_comb2"), sem("d_sum"))
            d_h, d_g, d_hi, d_loP, d_loD, d_y = sem("d_h"), sem("d_g"), sem("d_hi"), sem("d_loP"), sem("d_loD"), sem("d_y")
            o_out = sem("o_out")
            RSTEPS = 14
            RAW = 2
            ACC0 = E * NT

            LAST = NBLK * (L - 1)

            class Step:
                def __init__(self, eng, it, c):
                    self.n, self.m2 = 2 * it + c, c % 2
                    self.layer, self.block = self.n // NBLK, self.n % NBLK
                    if not isinstance(self.n, int):
                        self.layer, self.block = eng.snap(self.layer), eng.snap(self.block)
                    self.unit = E * self.n

                def expert(self, e):
                    return bass.ds(E * self.layer + e, 1)

                def tile(self, k):
                    return bass.ds(4 * self.block + k, 1)

            class Unit:
                def __init__(self, step, e):
                    self.step, self.e, self.n, self.m2 = step, e, step.unit + e, e % 2

            def steps(eng, unit, split=None, ready=None):
                SPLITS = (LE - E) // 2

                def run(it, c, final, prepare=True, attend=True, splits=False):
                    cur = Step(eng, it, c) if attend else None
                    nxt = Step(eng, it, c + 1) if prepare else None
                    before = None if isinstance(it, int) and c == 0 or not attend else Step(eng, it, c - 1) if isinstance(it, int) else \
                        Before(it, c - 1)
                    for e in range(E):
                        u = Unit(cur, e) if cur else None
                        v = Unit(cur, e - 1) if cur and e else Unit(before, E - 1) if before else None
                        unit(u, v, nxt, e, final)
                        if splits and split and e % 2 == 0:
                            split(eng, 2 * cur.n + (E - 2 + e // 2))

                class Before:
                    def __init__(self, it, c):
                        self.n, self.m2, self.unit = 2 * it + c, c % 2, E * (2 * it + c)
                        self.layer, self.block = self.n // NBLK, self.n % NBLK
                        self.expert = lambda e: bass.ds(E * self.layer + e, 1)
                        self.tile = lambda k: bass.ds(4 * self.block + k, 1)

                run(0, -1, False, attend=False)
                run(0, 0, False)
                with eng.Fori(0, SPLITS // 2) as it:
                    for k in range(2):
                        run(it, 1 + k, False, splits=True)
                if ready:
                    ready()
                with eng.Fori(SPLITS // 2, LAST // 2 - 1) as it:
                    for k in range(2):
                        run(it, 1 + k, False)
                with eng.Fori(LAST // 2 - 1, NSTEP // 2 - 1) as it:
                    for k in range(2):
                        run(it, 1 + k, True)
                run(0, NSTEP - 1, True, prepare=False)
                unit(None, Unit(Step(eng, 0, NSTEP - 1), E - 1), None, 0, True)

            with nc.Block() as block:
                @block.sync
                def _(sp):
                    for b in range(NBLK):
                        sp.wait_ge(d_acc, ACC0 + 4 * E * (LAST + b + 1))
                        sp.dma_start(out_tiles[:, 4 * b:4 * b + 4, :], hs[:, 4 * b:4 * b + 4, :]).then_inc(o_out, 16)
                    sp.wait_ge(o_out, 16 * NBLK)

                @block.gpsimd
                def _(pool):
                    def unit(u, v, f, e, final):
                        if u:
                            h = FC // 2
                            pool.wait_ge(d_hi, 2 * u.n + 1)
                            wait(pool, d_y, u.n - 1)
                            pool.tensor_tensor(gl[u.m2][:, 0:h, :], gf[u.m2][:, 0:h, :], gh[u.m2][:, 0:h, :],
                                               ALU.subtract).then_inc(d_loP, 1)
                    steps(pool, unit)

                @block.scalar
                def _(act):
                    def unit(u, v, f, e, final):
                        if u:
                            for c in range(FC):
                                act.wait_ge(d_h, FC * u.n + c + 1)
                                if c == 0:
                                    wait(act, d_loP, u.n - 1)
                                    wait(act, d_loD, u.n - 1)
                                act.activation(gf[u.m2][:, c, :], hb[c][:, :], ACT.Gelu, scale=1.0 / WS,
                                               bias=b1c[:, u.step.expert(u.e), c]).then_inc(d_g, 1)
                                if c % 2 == 1:
                                    wait(act, d_y, u.n - 1)
                                    act.wait_ge(d_g, FC * u.n + c + 1)
                                    act.activation(gh[u.m2][:, c - 1:c + 1, :], gf[u.m2][:, c - 1:c + 1, :],
                                                   ACT.Copy).then_inc(d_hi, 1)
                        if f and e == 1:
                            act.wait_ge(d_xT, f.n + 1)
                            wait(act, d_h, FC * E * (f.n - 1))
                            act.activation(xh[f.m2][:, :], tbk[:, :], ACT.Copy).then_inc(d_xh, 1)
                        if f and e == 3:
                            act.wait_ge(d_r, RSTEPS * (f.n + 1))
                            act.activation(th[:, :, :], z[:, :, :], ACT.Tanh).then_inc(d_th, 1)
                    steps(act, unit, high_weights)

                @block.vector
                def _(dve):
                    def normalise(f, final):
                        base = LNS * f.n
                        dve.wait_ge(d_acc, 4 * E * f.n + 4 * E)
                        for k in range(4):
                            dve.bn_stats(st4[:, k, :], hs[:, f.tile(k), :].rearrange("p a c -> p (a c)")).then_inc(d_ln, 1)
                        dve.wait_ge(d_ln, base + 4)
                        dve.memset(turn[:, :], 0.0)
                        for k in range(4):
                            dve.bn_aggr(mv4[:, k, :], st4[:, k, :]).then_inc(d_ln, 1)
                        dve.wait_ge(d_ln, base + 8)
                        inverse_deviation(dve, rs4[:, :], rw4[:, :], rt4[:, :], mv4[:, :, 1], d_ln, base + 8)
                        wait(dve, d_xT, f.n)
                        for k in range(4):
                            dve.tensor_scalar(xc[:, k, :], hs[:, f.tile(k), :].rearrange("p a c -> p (a c)"),
                                              mv4[:, k, 0:1], rs4[:, k:k + 1], ALU.subtract, ALU.mult).then_inc(d_x, 1)
                        if final:
                            blk = bass.ds(4 * f.block, 4)
                            dve.wait_ge(d_x, 4 * f.n + 4)
                            dve.tensor_tensor(hs[:, blk, :], hs[:, blk, :], xs[:, blk, :], ALU.add).then_inc(d_sum, 1)

                    def low_half(u):
                        h = FC // 2
                        dve.wait_ge(d_hi, 2 * u.n + 2)
                        wait(dve, d_y, u.n - 1)
                        dve.tensor_tensor(gl[u.m2][:, h:FC, :], gf[u.m2][:, h:FC, :], gh[u.m2][:, h:FC, :],
                                          ALU.subtract).then_inc(d_loD, 1)

                    def combine(v, final):
                        dve.wait_ge(d_y, v.n + 1)
                        dve.wait_ge(d_acc, 4 * v.n + ACC0)
                        dve.wait_ge(d_comb, v.step.n + 1)
                        if final and v.e == 0:
                            due = v.step.n - LAST + 2
                            dve.wait_ge(d_sum, min(due, NBLK) if isinstance(due, int) else due)
                        for k in range(4):
                            t = hs[:, v.step.tile(k), :].rearrange("p a c -> p (a c)")
                            dve.scalar_tensor_tensor(t, yb[v.m2][:, k * D:(k + 1) * D], comb[v.step.m2][:, k, v.e:v.e + 1],
                                                     t, ALU.mult, ALU.add).then_inc(d_acc, 1)

                    def route(f):
                        base = RSTEPS * f.n
                        wide = lambda t: t.unsqueeze(2).broadcast_to((P, 4, E))
                        per_layer = lambda t: t[:, bass.ds(f.layer, 1), :].broadcast_to((P, 4, E))
                        other = lambda t: t[:, :, :].unsqueeze(2).broadcast_to((P, 4, E, E))
                        own = lambda t: t[:, :, :].unsqueeze(3).broadcast_to((P, 4, E, E))
                        dve.tensor_tensor(sd4[:, :], rw4[:, :], rs4[:, :], ALU.mult).then_inc(d_r, 1)
                        dve.tensor_tensor(lc[:, :, :], wide(mv4[:, :, 0]), per_layer(srw), ALU.mult).then_inc(d_r, 1)
                        dve.wait_ge(d_r, base + 2)
                        dve.tensor_tensor(lc[:, :, :], lc[:, :, :], per_layer(rbR), ALU.add).then_inc(d_r, 1)
                        dve.wait_ge(d_lg, f.n + 1)
                        dve.tensor_tensor(lg[:, :, :], lbk[:, 0:4 * E].rearrange("p (t e) -> p t e", t=4), wide(sd4[:, :]),
                                          ALU.mult).then_inc(d_r, 1)
                        dve.wait_ge(d_r, base + 4)
                        dve.scalar_tensor_tensor(lg[:, :, :], lg[:, :, :], 1.0 / WS, lc[:, :, :], ALU.mult, ALU.add).then_inc(d_r, 1)
                        dve.wait_ge(d_r, base + 5)
                        dve.tensor_tensor(gt[:, :, :, :], other(lg), own(lg), ALU.is_gt).then_inc(d_r, 1)
                        dve.tensor_tensor(ge[:, :, :, :], other(lg), own(lg), ALU.is_ge).then_inc(d_r, 1)
                        dve.wait_ge(d_r, base + 7)
                        dve.tensor_tensor(ge[:, :, :, :], ge[:, :, :, :], lower[:, :, :].unsqueeze(1).broadcast_to((P, 4, E, E)),
                                          ALU.mult).then_inc(d_r, 1)
                        dve.wait_ge(d_r, base + 8)
                        dve.tensor_tensor(gt[:, :, :, :], gt[:, :, :, :], ge[:, :, :, :], ALU.max).then_inc(d_r, 1)
                        dve.wait_ge(d_r, base + 9)
                        dve.tensor_reduce(rank[:, :, :], gt[:, :, :, :], AX.X, ALU.add).then_inc(d_r, 1)
                        dve.wait_ge(d_r, base + 10)
                        dve.tensor_scalar(sel[:, :, :], rank[:, :, :], 1.5, None, ALU.is_lt).then_inc(d_r, 1)
                        dve.wait_ge(d_r, base + 11)
                        dve.tensor_tensor(sL[:, :, :], sel[:, :, :], lg[:, :, :], ALU.mult).then_inc(d_r, 1)
                        dve.wait_ge(d_r, base + 12)
                        dve.tensor_reduce(top[:, :], sL[:, :, :], AX.X, ALU.add).then_inc(d_r, 1)
                        dve.wait_ge(d_r, base + 13)
                        dve.scalar_tensor_tensor(z[:, :, :], wide(top[:, :]), -0.5, lg[:, :, :], ALU.mult, ALU.add).then_inc(d_r, 1)

                    def unit(u, v, f, e, final):
                        if f and e == 0:
                            normalise(f, final)
                        if u:
                            low_half(u)
                        if f and e == 1:
                            dve.wait_ge(d_xh, f.n + 1)
                            dve.tensor_tensor(xl[f.m2][:, :], tbk[:, :], xh[f.m2][:, :], ALU.subtract).then_inc(d_xl, 1)
                        if f and e == 2:
                            route(f)
                        if v:
                            combine(v, final)
                        if f and e == 3:
                            dve.tensor_scalar(sel2[:, :, :], sel[:, :, :], 0.5 / WS, None, ALU.mult).then_inc(d_comb2, 1)
                            dve.wait_ge(d_comb2, f.n + 1)
                            dve.wait_ge(d_th, f.n + 1)
                            dve.scalar_tensor_tensor(comb[f.m2][:, :, :], th[:, :, :], 1.0, sel2[:, :, :],
                                                     ALU.add, ALU.mult).then_inc(d_comb, 1)
                    steps(dve, unit, low_weights)

                @block.tensor
                def _(pe):
                    def hidden(u):
                        if u.e == 0:
                            pe.wait_ge(d_xl, u.step.n + 1)
                        x = (xh, xl, xh)
                        for c in range(FC):
                            wait(pe, d_g, FC * (u.n - 1) + c + 1)
                            for k, part in enumerate((0, 0, 1)):
                                last = pe.matmul(hb[c][:, :], w1p[:, u.step.expert(u.e), part, c * P:(c + 1) * P].rearrange("p a f -> p (a f)"),
                                                 x[k][u.step.m2][:, :], start=(k == 0), stop=(k == 2))
                            last.then_inc(d_h, 1)

                    def outputs(v):
                        wait(pe, d_acc, 4 * v.n + (ACC0 - 4))
                        le = v.step.expert(v.e)
                        pe.matmul(yb[v.m2][:, :], pick[:, le, :].rearrange("p a m -> p (a m)"),
                                  b2p[:, :].unsqueeze(1).broadcast_to((P, 4, D)), start=True, stop=False,
                                  skip_group_check=True)
                        for c in range(FC):
                            if c == 0:
                                pe.wait_ge(d_loP, v.n + 1)
                            if c == FC // 2:
                                pe.wait_ge(d_loD, v.n + 1)
                            for t in range(4):
                                for k, part in enumerate((0, 1, 0)):
                                    g = (gh, gh, gl)[k][v.m2]
                                    last = pe.matmul(yb[v.m2][:, t * D:(t + 1) * D], g[:, c, t * P:(t + 1) * P],
                                                     w2p[:, le, part, c, :].rearrange("p a h -> p (a h)"),
                                                     start=False, stop=(c == FC - 1 and k == 2), skip_group_check=True)
                        last.then_inc(d_y, 1)

                    def unit(u, v, f, e, final):
                        if u:
                            hidden(u)
                        if f and e == 1:
                            pe.wait_ge(d_x, 4 * f.n + 4)
                            wait(pe, d_xl, f.n)
                            for k in range(4):
                                last = pe.transpose(tbk[:, k * P:(k + 1) * P], xc[:, k, :], ident[:, :])
                            last.then_inc(d_xT, 1)
                        if f and e == 2:
                            pe.wait_ge(d_xl, f.n + 1)
                            wait(pe, d_r, RSTEPS * f.n)
                            for t in range(4):
                                for k, part in enumerate((0, 1, 0)):
                                    x = (xh, xh, xl)[k][f.m2]
                                    last = pe.matmul(lbk[:, t * E:(t + 1) * E], x[:, t * P:(t + 1) * P],
                                                     rwp[:, part, bass.ds(f.layer, 1), :].rearrange("p a e -> p (a e)"),
                                                     start=(k == 0), stop=(k == 2))
                            last.then_inc(d_lg, 1)
                        if v:
                            outputs(v)
                    def weights_ready():
                        pe.wait_ge(e_lo1, LE)
                        pe.wait_ge(e_lo2, LE)
                    steps(pe, unit, ready=weights_ready)



_INS = ['x', 'ctx_1024', 'mask_Bx1x1xS2_if1', 'L0_xattn_Wq', 'L0_xattn_bq', 'L0_xattn_Wk', 'L0_xattn_bk',
        'L0_xattn_Wv', 'L0_xattn_bv', 'L0_xattn_Wo', 'L0_xattn_bo', 'L0_attn_W_qkv', 'L0_attn_b_qkv',
        'L0_attn_W_out', 'L0_attn_b_out', 'L0_ffn_router_w', 'L0_ffn_router_b', 'L0_ffn_ln_g', 'L0_ffn_ln_b',
        'L0_ffn_w1', 'L0_ffn_b1', 'L0_ffn_w2', 'L0_ffn_b2']


def kernel(**inputs):
    import numpy as np
    import concourse.bacc as bacc
    from concourse.bass_utils import run_bass_kernel_spmd

    nc = bacc.Bacc("TRN2", target_bir_lowering=False, num_devices=1)
    arrays, args = {}, []
    for name in _INS:
        a = np.ascontiguousarray(inputs[name])
        arrays[f"in_{name}_dram"] = a
        args.append(nc.dram_tensor(f"in_{name}_dram", a.shape, mybir.dt.from_np(a.dtype), kind="ExternalInput").ap())
    shape = inputs["x"].shape
    args.append(nc.dram_tensor("out_dram", shape, F32, kind="ExternalOutput").ap())
    build(nc, *args)
    r = run_bass_kernel_spmd(nc, [arrays], core_ids=[0])
    return r.results[0]["out_dram"]
```
